# Optimizing a Trainium2 kernel written in Bass

```python
import numpy as np
import jax
import jax.numpy as jnp

def _softmax(x, axis=-1):
    return jax.nn.softmax(x, axis=axis)

def _gelu(x):
    return jax.nn.gelu(x, approximate=True)

def _silu(x):
    return jax.nn.silu(x)

def _sigmoid(x):
    return jax.nn.sigmoid(x)

def _layernorm(x, axis=-1, eps=1e-05):
    m = jnp.mean(x, axis=axis, keepdims=True)
    v = jnp.var(x, axis=axis, keepdims=True)
    return (x - m) / jnp.sqrt(v + eps)

def _scatter_add(tgt, idx, src, axis=0):
    return tgt.at[idx].add(src)

def _segment_sum(src, seg, n):
    return jax.ops.segment_sum(src, seg, n)
kernel_name = 'mk_conv_seq_d4_conv_nchw256_r2_b2a622'

def setup_inputs(seed: int=0):
    np.random.seed(seed)
    _w = jnp.asarray

    def _rec_inputs():
        import jax
        import jax.numpy as jnp
        _gk = jax.random.key(seed)
        x = -0.0002928 + 1 * jax.random.normal(jax.random.fold_in(_gk, 1), (4, 128, 32, 32), jnp.float32)
        return x
    x = _rec_inputs()

    def _L0_conv_setup():
        import jax, jax.numpy as jnp
        import numpy as np
        C_IN = 128
        C_RED = max(4, C_IN // 4)
        key = jax.random.key(seed)
        k1, k2, k3, k4, k5 = jax.random.split(key, 5)
        B, C, H, W = (4, C_IN, 32, 32)
        x = jax.random.normal(k1, (B, C, H, W), dtype=jnp.float32)
        s_in = 1.0 / np.sqrt(C)
        s_red = 1.0 / np.sqrt(C_RED)
        Wq = jax.random.normal(k2, (C_RED, C), dtype=jnp.float32) * s_in
        Wk = jax.random.normal(k3, (C_RED, C), dtype=jnp.float32) * s_in
        Wv = jax.random.normal(k4, (C_RED, C), dtype=jnp.float32) * s_in
        Wp = jax.random.normal(k5, (C, C_RED), dtype=jnp.float32) * s_red
        return {'x': x, 'Wq': Wq, 'Wk': Wk, 'Wv': Wv, 'Wp': Wp}
    _L0_conv_all = _L0_conv_setup()
    _L0_conv_in = {k: v for k, v in _L0_conv_all.items() if k in ('Wq', 'Wk', 'Wv', 'Wp')}
    del _L0_conv_all

    def _L1_conv_setup():
        import jax, jax.numpy as jnp
        import numpy as np
        EPS = 1e-05

        def _bn(x, g, b, m, v):
            s = g / jnp.sqrt(v + EPS)
            return x * s[None, :, None, None] + (b - m * s)[None, :, None, None]

        def _conv1x1(x, w):
            return jnp.einsum('bchw,oc->bohw', x, w)

        def _bilinear(img, y, x):
            B, C, Hi, Wi = img.shape
            y0 = jnp.floor(y)
            x0 = jnp.floor(x)
            wy1 = y - y0
            wx1 = x - x0
            wy0 = 1.0 - wy1
            wx0 = 1.0 - wx1
            imgf = img.reshape(B, C, Hi * Wi)

            def gather(yi, xi):
                valid = (yi >= 0) & (yi < Hi) & (xi >= 0) & (xi < Wi)
                yc = jnp.clip(yi, 0, Hi - 1).astype(jnp.int32)
                xc = jnp.clip(xi, 0, Wi - 1).astype(jnp.int32)
                flat = yc * Wi + xc

                def per_b(imgb, flatb):
                    return imgb[:, flatb.reshape(-1)].reshape(C, *flatb.shape)
                out = jax.vmap(per_b)(imgf, flat)
                return out * valid[:, None].astype(img.dtype)
            return gather(y0, x0) * (wy0 * wx0)[:, None] + gather(y0, x0 + 1) * (wy0 * wx1)[:, None] + gather(y0 + 1, x0) * (wy1 * wx0)[:, None] + gather(y0 + 1, x0 + 1) * (wy1 * wx1)[:, None]

        def _dcn(h, woff, boff, w2, b2):
            B, C, H, W = h.shape
            off = jax.lax.conv_general_dilated(h, woff, (1, 1), [(1, 1), (1, 1)], dimension_numbers=('NCHW', 'OIHW', 'NCHW')) + boff[None, :, None, None]
            o = off[:, :18].reshape(B, 9, 2, H, W)
            mask = jax.nn.sigmoid(off[:, 18:])
            ky, kx = jnp.meshgrid(jnp.arange(3), jnp.arange(3), indexing='ij')
            base_y = (jnp.arange(H)[None, :, None] - 1 + ky.reshape(9)[:, None, None]).astype(h.dtype)
            base_x = (jnp.arange(W)[None, None, :] - 1 + kx.reshape(9)[:, None, None]).astype(h.dtype)
            y = o[:, :, 0] + base_y[None]
            x = o[:, :, 1] + base_x[None]
            samp = _bilinear(h, y, x) * mask[:, None]
            out = jnp.einsum('bckhw,ock->bohw', samp, w2.reshape(w2.shape[0], w2.shape[1], 9))
            return out + b2[None, :, None, None]
        key = jax.random.key(seed)
        ks = jax.random.split(key, 20)
        B, Cin, Cb, H, W = (4, 128, 32, 56, 56)
        d = {'x': jax.random.normal(ks[0], (B, Cin, H, W), jnp.float32), 'w1': jax.random.normal(ks[1], (Cb, Cin), jnp.float32) * 0.05, 'bn1_g': jax.random.uniform(ks[2], (Cb,), jnp.float32, 0.5, 1.5), 'bn1_b': jax.random.normal(ks[3], (Cb,), jnp.float32) * 0.1, 'bn1_m': jax.random.normal(ks[4], (Cb,), jnp.float32) * 0.1, 'bn1_v': jax.random.uniform(ks[5], (Cb,), jnp.float32, 0.5, 1.5), 'woff': jax.random.normal(ks[6], (27, Cb, 3, 3), jnp.float32) * 0.01, 'boff': jax.random.normal(ks[7], (27,), jnp.float32) * 0.1, 'w2': jax.random.normal(ks[8], (Cb, Cb, 3, 3), jnp.float32) * 0.05, 'dcn_b': jax.random.normal(ks[9], (Cb,), jnp.float32) * 0.1, 'bn2_g': jax.random.uniform(ks[10], (Cb,), jnp.float32, 0.5, 1.5), 'bn2_b': jax.random.normal(ks[11], (Cb,), jnp.float32) * 0.1, 'bn2_m': jax.random.normal(ks[12], (Cb,), jnp.float32) * 0.1, 'bn2_v': jax.random.uniform(ks[13], (Cb,), jnp.float32, 0.5, 1.5), 'w3': jax.random.normal(ks[14], (Cin, Cb), jnp.float32) * 0.05, 'bn3_g': jax.random.uniform(ks[15], (Cin,), jnp.float32, 0.5, 1.5), 'bn3_b': jax.random.normal(ks[16], (Cin,), jnp.float32) * 0.1, 'bn3_m': jax.random.normal(ks[17], (Cin,), jnp.float32) * 0.1, 'bn3_v': jax.random.uniform(ks[18], (Cin,), jnp.float32, 0.5, 1.5)}
        return d
    _L1_conv_all = _L1_conv_setup()
    _L1_conv_in = {k: v for k, v in _L1_conv_all.items() if k in ('w1', 'bn1_g', 'bn1_b', 'bn1_m', 'bn1_v', 'woff', 'boff', 'w2', 'dcn_b', 'bn2_g', 'bn2_b', 'bn2_m', 'bn2_v', 'w3', 'bn3_g', 'bn3_b', 'bn3_m', 'bn3_v')}
    del _L1_conv_all

    def _L2_conv_setup():
        import jax, jax.numpy as jnp
        import numpy as np
        NI = 128
        QK = NI // 8
        BS, H, W = (4, 32, 32)
        key = jax.random.key(seed)
        ks = jax.random.split(key, 8)
        x = jax.random.normal(ks[0], (BS, NI, H, W), dtype=jnp.float32)
        wq = jax.random.normal(ks[1], (QK, NI), dtype=jnp.float32) * (1.0 / np.sqrt(NI))
        bq = jnp.zeros((QK,), dtype=jnp.float32)
        wk = jax.random.normal(ks[2], (QK, NI), dtype=jnp.float32) * (1.0 / np.sqrt(NI))
        bk = jnp.zeros((QK,), dtype=jnp.float32)
        wv = jax.random.normal(ks[3], (NI, NI), dtype=jnp.float32) * (1.0 / np.sqrt(NI))
        bv = jnp.zeros((NI,), dtype=jnp.float32)
        gamma = jax.random.normal(ks[4], (1, NI, 1, 1), dtype=jnp.float32) * 0.1
        return {'x': x, 'wq': wq, 'bq': bq, 'wk': wk, 'bk': bk, 'wv': wv, 'bv': bv, 'gamma': gamma}
    _L2_conv_all = _L2_conv_setup()
    _L2_conv_in = {k: v for k, v in _L2_conv_all.items() if k in ('wq', 'bq', 'wk', 'bk', 'wv', 'bv', 'gamma')}
    del _L2_conv_all

    def _L3_conv_setup():
        import jax, jax.numpy as jnp
        import numpy as np
        import math
        GROUPS = 32
        EPS = 1e-05

        def group_norm(x, w, b):
            B, C, H, W = x.shape
            xg = x.reshape(B, GROUPS, C // GROUPS, H, W)
            mean = jnp.mean(xg, axis=(2, 3, 4), keepdims=True)
            var = jnp.var(xg, axis=(2, 3, 4), keepdims=True)
            xn = ((xg - mean) * jax.lax.rsqrt(var + EPS)).reshape(B, C, H, W)
            return xn * w[None, :, None, None] + b[None, :, None, None]

        def nin(x, W, b):
            return jnp.einsum('bchw,cd->bdhw', x, W) + b[None, :, None, None]
        key = jax.random.key(seed)
        ks = jax.random.split(key, 5)
        C = 128
        scale = 1.0 / math.sqrt(C)
        return {'x': jax.random.normal(ks[0], (4, C, 32, 32), dtype=jnp.float32), 'gn_w': jnp.ones((C,), jnp.float32), 'gn_b': jnp.zeros((C,), jnp.float32), 'Wq': jax.random.normal(ks[1], (C, C), jnp.float32) * scale, 'bq': jnp.zeros((C,), jnp.float32), 'Wk': jax.random.normal(ks[2], (C, C), jnp.float32) * scale, 'bk': jnp.zeros((C,), jnp.float32), 'Wv': jax.random.normal(ks[3], (C, C), jnp.float32) * scale, 'bv': jnp.zeros((C,), jnp.float32), 'Wp': jax.random.normal(ks[4], (C, C), jnp.float32) * scale, 'bp': jnp.zeros((C,), jnp.float32)}
    _L3_conv_all = _L3_conv_setup()
    _L3_conv_in = {k: v for k, v in _L3_conv_all.items() if k in ('gn_w', 'gn_b', 'Wq', 'bq', 'Wk', 'bk', 'Wv', 'bv', 'Wp', 'bp')}
    del _L3_conv_all
    return {'x': x, 'L0_conv_Wq': _L0_conv_in['Wq'], 'L0_conv_Wk': _L0_conv_in['Wk'], 'L0_conv_Wv': _L0_conv_in['Wv'], 'L0_conv_Wp': _L0_conv_in['Wp'], 'L1_conv_w1': _L1_conv_in['w1'], 'L1_conv_bn1_g': _L1_conv_in['bn1_g'], 'L1_conv_bn1_b': _L1_conv_in['bn1_b'], 'L1_conv_bn1_m': _L1_conv_in['bn1_m'], 'L1_conv_bn1_v': _L1_conv_in['bn1_v'], 'L1_conv_woff': _L1_conv_in['woff'], 'L1_conv_boff': _L1_conv_in['boff'], 'L1_conv_w2': _L1_conv_in['w2'], 'L1_conv_dcn_b': _L1_conv_in['dcn_b'], 'L1_conv_bn2_g': _L1_conv_in['bn2_g'], 'L1_conv_bn2_b': _L1_conv_in['bn2_b'], 'L1_conv_bn2_m': _L1_conv_in['bn2_m'], 'L1_conv_bn2_v': _L1_conv_in['bn2_v'], 'L1_conv_w3': _L1_conv_in['w3'], 'L1_conv_bn3_g': _L1_conv_in['bn3_g'], 'L1_conv_bn3_b': _L1_conv_in['bn3_b'], 'L1_conv_bn3_m': _L1_conv_in['bn3_m'], 'L1_conv_bn3_v': _L1_conv_in['bn3_v'], 'L2_conv_wq': _L2_conv_in['wq'], 'L2_conv_bq': _L2_conv_in['bq'], 'L2_conv_wk': _L2_conv_in['wk'], 'L2_conv_bk': _L2_conv_in['bk'], 'L2_conv_wv': _L2_conv_in['wv'], 'L2_conv_bv': _L2_conv_in['bv'], 'L2_conv_gamma': _L2_conv_in['gamma'], 'L3_conv_gn_w': _L3_conv_in['gn_w'], 'L3_conv_gn_b': _L3_conv_in['gn_b'], 'L3_conv_Wq': _L3_conv_in['Wq'], 'L3_conv_bq': _L3_conv_in['bq'], 'L3_conv_Wk': _L3_conv_in['Wk'], 'L3_conv_bk': _L3_conv_in['bk'], 'L3_conv_Wv': _L3_conv_in['Wv'], 'L3_conv_bv': _L3_conv_in['bv'], 'L3_conv_Wp': _L3_conv_in['Wp'], 'L3_conv_bp': _L3_conv_in['bp']}

def reference(x, L0_conv_Wq, L0_conv_Wk, L0_conv_Wv, L0_conv_Wp, L1_conv_w1, L1_conv_bn1_g, L1_conv_bn1_b, L1_conv_bn1_m, L1_conv_bn1_v, L1_conv_woff, L1_conv_boff, L1_conv_w2, L1_conv_dcn_b, L1_conv_bn2_g, L1_conv_bn2_b, L1_conv_bn2_m, L1_conv_bn2_v, L1_conv_w3, L1_conv_bn3_g, L1_conv_bn3_b, L1_conv_bn3_m, L1_conv_bn3_v, L2_conv_wq, L2_conv_bq, L2_conv_wk, L2_conv_bk, L2_conv_wv, L2_conv_bv, L2_conv_gamma, L3_conv_gn_w, L3_conv_gn_b, L3_conv_Wq, L3_conv_bq, L3_conv_Wk, L3_conv_bk, L3_conv_Wv, L3_conv_bv, L3_conv_Wp, L3_conv_bp):
    import jax
    import jax.numpy as jnp

    def _L0_conv_ref(x, Wq, Wk, Wv, Wp):
        import jax, jax.numpy as jnp
        import numpy as np
        C_IN = 128
        C_RED = max(4, C_IN // 4)
        B, C, H, W = x.shape
        N = H * W
        xf = x.reshape(B, C, N)
        q = jnp.einsum('rc,bcn->bnr', Wq, xf)
        k = jnp.einsum('rc,bcn->brn', Wk, xf)
        v = jnp.einsum('rc,bcn->bnr', Wv, xf)
        scale = 1.0 / jnp.sqrt(jnp.float32(k.shape[1]))
        attn = jnp.einsum('bnr,brm->bnm', q, k) * scale
        attn = jax.nn.softmax(attn, axis=-1)
        out = jnp.einsum('bnm,bmr->brn', attn, v)
        out = jnp.einsum('cr,brn->bcn', Wp, out)
        return out.reshape(B, C, H, W) + x

    def _L1_conv_ref(x, w1, bn1_g, bn1_b, bn1_m, bn1_v, woff, boff, w2, dcn_b, bn2_g, bn2_b, bn2_m, bn2_v, w3, bn3_g, bn3_b, bn3_m, bn3_v):
        import jax, jax.numpy as jnp
        import numpy as np
        EPS = 1e-05

        def _bn(x, g, b, m, v):
            s = g / jnp.sqrt(v + EPS)
            return x * s[None, :, None, None] + (b - m * s)[None, :, None, None]

        def _conv1x1(x, w):
            return jnp.einsum('bchw,oc->bohw', x, w)

        def _bilinear(img, y, x):
            B, C, Hi, Wi = img.shape
            y0 = jnp.floor(y)
            x0 = jnp.floor(x)
            wy1 = y - y0
            wx1 = x - x0
            wy0 = 1.0 - wy1
            wx0 = 1.0 - wx1
            imgf = img.reshape(B, C, Hi * Wi)

            def gather(yi, xi):
                valid = (yi >= 0) & (yi < Hi) & (xi >= 0) & (xi < Wi)
                yc = jnp.clip(yi, 0, Hi - 1).astype(jnp.int32)
                xc = jnp.clip(xi, 0, Wi - 1).astype(jnp.int32)
                flat = yc * Wi + xc

                def per_b(imgb, flatb):
                    return imgb[:, flatb.reshape(-1)].reshape(C, *flatb.shape)
                out = jax.vmap(per_b)(imgf, flat)
                return out * valid[:, None].astype(img.dtype)
            return gather(y0, x0) * (wy0 * wx0)[:, None] + gather(y0, x0 + 1) * (wy0 * wx1)[:, None] + gather(y0 + 1, x0) * (wy1 * wx0)[:, None] + gather(y0 + 1, x0 + 1) * (wy1 * wx1)[:, None]

        def _dcn(h, woff, boff, w2, b2):
            B, C, H, W = h.shape
            off = jax.lax.conv_general_dilated(h, woff, (1, 1), [(1, 1), (1, 1)], dimension_numbers=('NCHW', 'OIHW', 'NCHW')) + boff[None, :, None, None]
            o = off[:, :18].reshape(B, 9, 2, H, W)
            mask = jax.nn.sigmoid(off[:, 18:])
            ky, kx = jnp.meshgrid(jnp.arange(3), jnp.arange(3), indexing='ij')
            base_y = (jnp.arange(H)[None, :, None] - 1 + ky.reshape(9)[:, None, None]).astype(h.dtype)
            base_x = (jnp.arange(W)[None, None, :] - 1 + kx.reshape(9)[:, None, None]).astype(h.dtype)
            y = o[:, :, 0] + base_y[None]
            x = o[:, :, 1] + base_x[None]
            samp = _bilinear(h, y, x) * mask[:, None]
            out = jnp.einsum('bckhw,ock->bohw', samp, w2.reshape(w2.shape[0], w2.shape[1], 9))
            return out + b2[None, :, None, None]
        h = jax.nn.relu(_bn(_conv1x1(x, w1), bn1_g, bn1_b, bn1_m, bn1_v))
        h = _dcn(h, woff, boff, w2, dcn_b)
        h = jax.nn.relu(_bn(h, bn2_g, bn2_b, bn2_m, bn2_v))
        h = _bn(_conv1x1(h, w3), bn3_g, bn3_b, bn3_m, bn3_v)
        return jax.nn.relu(h + x)

    def _L2_conv_ref(x, wq, bq, wk, bk, wv, bv, gamma):
        import jax, jax.numpy as jnp
        import numpy as np
        NI = 128
        QK = NI // 8
        BS, H, W = (4, 32, 32)
        bs, c, h, w = x.shape
        n = h * w
        xf = x.reshape(bs, c, n)
        q = jnp.einsum('oc,bcn->bno', wq, xf) + bq
        k = jnp.einsum('oc,bcn->bon', wk, xf) + bk[None, :, None]
        v = jnp.einsum('oc,bcn->bon', wv, xf) + bv[None, :, None]
        attn = jax.nn.softmax(jnp.einsum('bnq,bqm->bnm', q, k), axis=-1)
        out = jnp.einsum('bcm,bnm->bcn', v, attn)
        out = out.reshape(bs, c, h, w)
        return gamma * out + x

    def _L3_conv_ref(x, gn_w, gn_b, Wq, bq, Wk, bk, Wv, bv, Wp, bp):
        import jax, jax.numpy as jnp
        import numpy as np
        import math
        GROUPS = 32
        EPS = 1e-05

        def group_norm(x, w, b):
            B, C, H, W = x.shape
            xg = x.reshape(B, GROUPS, C // GROUPS, H, W)
            mean = jnp.mean(xg, axis=(2, 3, 4), keepdims=True)
            var = jnp.var(xg, axis=(2, 3, 4), keepdims=True)
            xn = ((xg - mean) * jax.lax.rsqrt(var + EPS)).reshape(B, C, H, W)
            return xn * w[None, :, None, None] + b[None, :, None, None]

        def nin(x, W, b):
            return jnp.einsum('bchw,cd->bdhw', x, W) + b[None, :, None, None]
        B, C, H, W = x.shape
        h = group_norm(x, gn_w, gn_b)
        q = nin(h, Wq, bq).reshape(B, C, H * W)
        k = nin(h, Wk, bk).reshape(B, C, H * W)
        v = nin(h, Wv, bv).reshape(B, C, H * W)
        w = jnp.einsum('bcn,bcm->bnm', q, k) * C ** (-0.5)
        w = jax.nn.softmax(w, axis=-1)
        h_out = jnp.einsum('bnm,bcm->bcn', w, v).reshape(B, C, H, W)
        h_out = nin(h_out, Wp, bp)
        out = x + h_out
        return out / math.sqrt(2.0)

    def _gn(v, G=32, eps=1e-05):
        B_, C_, H_, W_ = v.shape
        g = v.reshape(B_, G, C_ // G, H_, W_)
        m = jnp.mean(g, axis=(2, 3, 4), keepdims=True)
        s = jnp.var(g, axis=(2, 3, 4), keepdims=True)
        return ((g - m) / jnp.sqrt(s + eps)).reshape(v.shape)

    def _ln_c(v, eps=1e-06):
        m = jnp.mean(v, axis=1, keepdims=True)
        s = jnp.var(v, axis=1, keepdims=True)
        return (v - m) / jnp.sqrt(s + eps)

    def _ln_t(v, eps=1e-05):
        m = jnp.mean(v, axis=-1, keepdims=True)
        s = jnp.var(v, axis=-1, keepdims=True)
        return (v - m) / jnp.sqrt(s + eps)

    def _to_tokens(v):
        B_, C_, H_, W_ = v.shape
        return v.reshape(B_, C_, H_ * W_).transpose(0, 2, 1)

    def _from_tokens(t, like):
        B_, C_, H_, W_ = like.shape
        return t.transpose(0, 2, 1).reshape(B_, C_, H_, W_)
    x = _L0_conv_ref(x, L0_conv_Wq, L0_conv_Wk, L0_conv_Wv, L0_conv_Wp)
    x = _L1_conv_ref(x, L1_conv_w1, L1_conv_bn1_g, L1_conv_bn1_b, L1_conv_bn1_m, L1_conv_bn1_v, L1_conv_woff, L1_conv_boff, L1_conv_w2, L1_conv_dcn_b, L1_conv_bn2_g, L1_conv_bn2_b, L1_conv_bn2_m, L1_conv_bn2_v, L1_conv_w3, L1_conv_bn3_g, L1_conv_bn3_b, L1_conv_bn3_m, L1_conv_bn3_v)
    x = _L2_conv_ref(x, L2_conv_wq, L2_conv_bq, L2_conv_wk, L2_conv_bk, L2_conv_wv, L2_conv_bv, L2_conv_gamma)
    x = _L3_conv_ref(x, L3_conv_gn_w, L3_conv_gn_b, L3_conv_Wq, L3_conv_bq, L3_conv_Wk, L3_conv_bk, L3_conv_Wv, L3_conv_bv, L3_conv_Wp, L3_conv_bp)
    return x

_drawn_inputs = setup_inputs


def setup_inputs(seed=0):
    import zlib

    import numpy as np

    out = dict(_drawn_inputs(seed))
    spreads = {'L2_conv_bq': (0.0, 0.8),
     'L2_conv_bk': (0.0, 0.8),
     'L2_conv_bv': (0.0, 0.338),
     'L3_conv_gn_w': (1.0, 0.2),
     'L3_conv_gn_b': (0.0, 0.1),
     'L3_conv_bq': (0.0, 0.495),
     'L3_conv_bk': (0.0, 0.8),
     'L3_conv_bv': (0.0, 0.1),
     'L3_conv_bp': (0.0, 0.1)}
    factors = {'L1_conv_bn1_g': 5.647,
     'L1_conv_bn1_b': 7.265,
     'L1_conv_bn1_m': 8.0,
     'L1_conv_bn1_v': 8.0,
     'L1_conv_woff': 8.0,
     'L1_conv_boff': 8.0,
     'L1_conv_bn2_g': 2.908,
     'L1_conv_bn2_v': 5.369,
     'L2_conv_wk': 2.848}
    for name, (base, spread) in spreads.items():
        noise = np.random.default_rng([zlib.crc32(name.encode()), seed]).standard_normal(out[name].shape)
        drawn = base * np.exp(spread * noise) if base else spread * noise
        out[name] = jnp.asarray(drawn.astype(out[name].dtype))
    for name, factor in factors.items():
        out[name] = (out[name] * factor).astype(out[name].dtype)
    return out
```

```python
import numpy as np
import concourse.bass as bass
from concourse import mybir
from contextlib import ExitStack

BATCH, C, H, W = 4, 128, 32, 32
N = H * W
P = 128
TILES = N // P
ROWS = P // W
HALF = 512
R = 32
QK2 = C // 8
TAPS = 9
CORNERS = 4
GROUP = C // 32
EPS = 1e-5
CELLS = H + 1
TABLE = CELLS * CELLS
TCHUNKS = -(-TABLE // P)
TLAST = TABLE - (TCHUNKS - 1) * P
YX = 2 * TAPS
OFFS = 3 * TAPS
TAPS_A_TURN = 3
TURNS = TAPS // TAPS_A_TURN
TR = TAPS_A_TURN * R
ROUND = 1.5 * 2 ** 23

COLUMNS = [
    ("ident", P), ("wq0", P), ("wk0", P), ("wv0", R), ("wp0", P),
    ("w1", P), ("bn_g", 3), ("bn_b", 3), ("bn_m", 3), ("bn_v", 3), ("dcn_b", 1),
    ("woff", 4 * R), ("boff", 1), ("osum", OFFS), ("base", TILES * YX), ("w2", TURNS * P), ("w3", P),
    ("wq2", P), ("wk2", P), ("wv2", C), ("bq2", 1), ("bk2", 1), ("bv2", C), ("gamma", 1),
    ("wq3", C), ("wk3", C), ("wvT3", C), ("wp3", C), ("bq3", 1), ("bk3", 1), ("bv3", P), ("bp3", 1),
    ("gn_w", 1), ("gn_b", 1), ("gavg", P),
]
AT, _at = {}, 0
for _name, _width in COLUMNS:
    AT[_name] = (_at, _at + _width)
    _at += _width
WIDTH = _at
FIRST = AT["w1"][0]


class Layer:
    def __init__(self, sem, n):
        self.n = n
        self.x_ready = sem(f"x_ready_{n}")
        self.q_mm = sem(f"q_mm_{n}")
        self.k_mm = sem(f"k_mm_{n}")
        self.v_mm = sem(f"v_mm_{n}")
        self.q_high = sem(f"q_high_{n}")
        self.k_high = sem(f"k_high_{n}")
        self.q_ready = sem(f"q_ready_{n}")
        self.k_ready = sem(f"k_ready_{n}")
        self.v_ready = sem(f"v_ready_{n}")
        self.s_mm = sem(f"s_mm_{n}")
        self.max_done = sem(f"max_done_{n}")
        self.exp_done = sem(f"exp_done_{n}")
        self.pt_mm = sem(f"pt_mm_{n}")
        self.pt_act = sem(f"pt_act_{n}")
        self.pt_dve = sem(f"pt_dve_{n}")
        self.inv_done = sem(f"inv_done_{n}")
        self.o_mm = sem(f"o_mm_{n}")
        self.o_norm = sem(f"o_norm_{n}")
        self.ot_mm = sem(f"ot_mm_{n}")


def build(nc, x_dram, weights_dram, out_dram):
    fp32, fp32r, int32 = mybir.dt.float32, mybir.dt.float32r, mybir.dt.int32
    ALU, ACT, X = mybir.AluOpType, mybir.ActivationFunctionType, mybir.AxisListType.X
    x_view = x_dram.rearrange("b c h w -> b c (h w)")
    out_view = out_dram.rearrange("b c h w -> b c (h w)")
    ctx = ExitStack()
    with ctx:
        def sb(name, shape, dt=fp32):
            return ctx.enter_context(nc.sbuf_tensor(name, shape, dt))

        def sem(name):
            return ctx.enter_context(nc.semaphore(name))

        tables = [nc.dram_tensor(f"cell_table{n}", (TABLE, CORNERS * R), fp32).ap() for n in range(2)]

        wts = sb("wts", [P, WIDTH])

        def wt(name, rows=P):
            a, b = AT[name]
            return wts[0:rows, a:b]

        ident = wt("ident")
        xall = sb("xall", [P, BATCH, N])
        xcur = sb("xcur", [P, N])
        x2 = sb("x2", [P, N])
        x3 = sb("x3", [P, N])
        h3 = sb("h3", [P, N])
        q_stack = sb("q_stack", [P, N], fp32r)
        k_stack = sb("k_stack", [P, N], fp32r)
        q3 = sb("q3", [P, N])
        k3 = sb("k3", [P, N])
        vT = sb("vT", [P, TILES, C])
        probs = sb("probs", [P, 2, N])
        probsT = sb("probsT", [P, 2, N])
        neg_max = sb("neg_max", [P, TILES])
        denom = sb("denom", [P, TILES])
        inv_denom = sb("inv_denom", [P, TILES])
        oT = sb("oT", [P, TILES, C])
        o_stack = sb("o_stack", [P, N], fp32r)
        wp0_stack = sb("wp0_stack", [P, P], fp32r)
        w3_stack = sb("w3_stack", [P, P], fp32r)
        bn_std = sb("bn_std", [P, 3])
        bn_s = sb("bn_s", [P, 3])
        bn_t = sb("bn_t", [P, 3])
        cells = sb("cells", [P, CELLS, CELLS])
        tabS = sb("tabS", [P, BATCH, TCHUNKS, P])
        offs4 = sb("offs4", [P, N])
        offs = sb("offs", [P, TILES, OFFS])
        yx = sb("yx", [P, TILES, YX])
        low = sb("low", [P, TILES, YX])
        frac = sb("frac", [P, TILES, YX])
        rest = sb("rest", [P, TILES, YX])
        mask = sb("mask", [P, TILES, TAPS])
        mexp = sb("mexp", [P, TILES, TAPS])
        wy = sb("wy", [P, 2, TILES, TAPS])
        rows_all = sb("rows_all", [P, BATCH, TILES * TAPS], int32)
        rows_cur = sb("rows_cur", [P, 2, TILES * TAPS], int32)
        corner_w = sb("corner_w", [P, BATCH, TILES, TAPS * CORNERS])
        got = sb("got", [P, TILES, TAPS, CORNERS * R])
        weighed = sb("weighed", [P, 2, TAPS, CORNERS * R])
        samples = sb("samples", [P, 2, TAPS * R])
        samplesT = sb("samplesT", [TR, TURNS, N])
        h2_stack = sb("h2_stack", [P, N], fp32r)
        h2_full = sb("h2_full", [P, N])
        x2_sum = sb("x2_sum", [P, N])
        stats = sb("stats", [P, 2, 6])
        mom = sb("mom", [P, 2])
        gmom = sb("gmom", [P, 2])
        gsq = sb("gsq", [P, 1])
        gvar = sb("gvar", [P, 1])
        gstd = sb("gstd", [P, 1])
        gscale = sb("gscale", [P, 1])
        gbias = sb("gbias", [P, 1])
        u3 = sb("u3", [P, C])
        bvp3 = sb("bvp3", [P, C])
        bq3s = sb("bq3s", [P, 1])
        bp3s = sb("bp3s", [P, 1])
        x3s = sb("x3s", [P, N])
        y = sb("y", [P, N])

        pa = ctx.enter_context(nc.psum_tensor("pa", [P, N], fp32))
        pb = ctx.enter_context(nc.psum_tensor("pb", [P, N], fp32))
        pc = ctx.enter_context(nc.psum_tensor("pc", [P, N], fp32))
        pd = ctx.enter_context(nc.psum_tensor("pd", [P, HALF], fp32))
        pe_ = ctx.enter_context(nc.psum_tensor("pe", [P, HALF], fp32))
        scores_bank = [pa, pb]
        single = [pd, pe_]

        weights0_in = sem("weights0_in")
        weights_in = sem("weights_in")
        x_in_sem = [sem(f"x_in{b}") for b in range(BATCH)]
        setup_sqrt = sem("setup_sqrt")
        setup_dve = sem("setup_dve")
        setup_pe = sem("setup_pe")
        setup_act = sem("setup_act")

        L0, L2, L3 = Layer(sem, 0), Layer(sem, 2), Layer(sem, 3)
        o_high = sem("o_high")
        o_split = sem("o_split")
        wp_mm = sem("wp_mm")
        x1_ready = sem("x1_ready")
        conv1_mm = sem("conv1_mm")
        cells_done = sem("cells_done")
        off4_mm = sem("off4_mm")
        off4_copied = sem("off4_copied")
        off_mm = sem("off_mm")
        off_read = sem("off_read")
        mask_exp = sem("mask_exp")
        rows_ready = sem("rows_ready")
        corner_ready = sem("corner_ready")
        tab_mm = sem("tab_mm")
        tab_copied = sem("tab_copied")
        tab_out = [sem(f"tab_out{n}") for n in range(2)]
        rows_copied = sem("rows_copied")
        sp_go = sem("sp_go")
        pool_go = sem("pool_go")
        got_sem = [sem(f"got{t}") for t in range(TILES)]
        slot_free = sem("slot_free")
        weighed_sem = sem("weighed_sem")
        sample_ready = sem("sample_ready")
        st_mm = sem("st_mm")
        st_copied = sem("st_copied")
        w2_mm = sem("w2_mm")
        h2_high = sem("h2_high")
        h2_split = sem("h2_split")
        w3_mm = sem("w3_mm")
        x2_added = sem("x2_added")
        mom_ready = sem("mom_ready")
        g_mm = sem("g_mm")
        gvar_ready = sem("gvar_ready")
        gstd_ready = sem("gstd_ready")
        gaff_ready = sem("gaff_ready")
        x3s_ready = sem("x3s_ready")
        y_ready = sem("y_ready")
        y_out = sem("y_out")

        block = ctx.enter_context(nc.Block())

        @block.sync
        def _(sp):
            sp.dma_start(wts[:, 0:FIRST], weights_dram[:, 0:FIRST]).then_inc(weights0_in, 16)
            for b in range(1, BATCH):
                sp.dma_start(xall[:, b, :], x_view[b]).then_inc(x_in_sem[b], 16)
            tab_pair = tabS[:, :, :, :].rearrange("p (a n) k d -> p a n k d", n=2)
            with sp.Fori(0, BATCH // 2) as i:
                for n, table in enumerate(tables):
                    sp.wait_ge(tab_copied, 6 * i + 3 * n + 3)
                    sp.sem_inc(sp_go, 1)
                    sp.wait_ge(slot_free, 2 * TILES * i + TILES * n)
                    sp.dma_start(table[0:(TCHUNKS - 1) * P, :].rearrange("(k p) d -> p k d", p=P),
                                 tab_pair[:, bass.ds(i, 1), n, 0:TCHUNKS - 1, :].rearrange("p a k d -> p (a k) d"))\
                        .then_inc(tab_out[n], 16)
                    sp.dma_start(table[(TCHUNKS - 1) * P:TABLE, :], 
                                 tab_pair[0:TLAST, bass.ds(i, 1), n, TCHUNKS - 1, :].rearrange("p a d -> p (a d)"))\
                        .then_inc(tab_out[n], 16)
            with sp.Fori(0, BATCH) as i:
                sp.wait_ge(y_ready, i + 1)
                sp.sem_inc(sp_go, 1)
                sp.dma_start(out_view[bass.ds(i, 1), :, :].rearrange("b c n -> (b c) n"), y[:, :]).then_inc(y_out, 16)
            sp.wait_ge(y_out, 16 * BATCH)
            for n in range(2):
                sp.wait_ge(tab_out[n], 16 * BATCH)

        @block.gpsimd
        def _(pool):
            with pool.Fori(0, BATCH // 2) as i:
                for n, table in enumerate(tables):
                    pool.wait_ge(rows_ready, 2 * i + n + 1)
                    nc.gpsimd.tensor_copy(rows_cur[:, n, :], rows_all[:, :, :].rearrange("p (a b) n -> p a b n", b=2)[:, bass.ds(i, 1), n, :].rearrange("p a n -> p (a n)"))\
                        .then_inc(rows_copied, 1)
                    pool.wait_ge(rows_copied, 2 * i + n + 1)
                    pool.wait_ge(tab_out[n], 32 * i + 32)
                    for t in range(TILES):
                        pool.wait_ge(slot_free, 2 * TILES * i + TILES * n + t + 1)
                        pool.sem_inc(pool_go, 1)
                        for k in range(TAPS):
                            at = t * TAPS + k
                            nc.gpsimd.indirect_dma_start(
                                got[:, t, k, :], None, table,
                                bass.IndirectOffsetOnAxis(ap=rows_cur[:, n, at:at + 1], axis=0)).then_inc(got_sem[t], 16)

        def scores(L, t, q, k):
            for h in range(2):
                last = nc.tensor.matmul(scores_bank[t % 2][:, h * HALF:(h + 1) * HALF], q[:, t * P:(t + 1) * P],
                                        k[:, h * HALF:(h + 1) * HALF], start=True, stop=True)
            last.then_inc(L.s_mm, 1)

        def pe_attention(pe, L, i, x, wq, wk, wv, q, k, width):
            pe.wait_ge(L.x_ready, i + 1)
            for w, bank, done in ((wq, pa, L.q_mm), (wk, pb, L.k_mm)):
                for h in range(2):
                    last = nc.tensor.matmul(bank[:, h * HALF:(h + 1) * HALF], w, x[:, h * HALF:(h + 1) * HALF],
                                            start=True, stop=True)
                last.then_inc(done, 1)
            for j in range(TILES):
                last = nc.tensor.matmul(pc[:, j * width:(j + 1) * width], x[:, j * P:(j + 1) * P], wv,
                                        start=True, stop=True)
            last.then_inc(L.v_mm, 1)
            pe.wait_ge(L.q_ready, i + 1)
            pe.wait_ge(L.k_ready, i + 1)
            scores(L, 0, q, k)
            scores(L, 1, q, k)
            pe.wait_ge(L.v_ready, i + 1)

            def weigh_values(t):
                if t >= 2:
                    pe.wait_ge(L.o_norm, TILES * i + t - 1)
                for j in range(TILES):
                    last = nc.tensor.matmul(single[t % 2][:, 0:width], probsT[:, t % 2, j * P:(j + 1) * P],
                                            vT[:, j, 0:width], start=j == 0, stop=j == TILES - 1)
                last.then_inc(L.o_mm, 1)

            for t in range(TILES):
                pe.wait_ge(L.exp_done, TILES * i + t + 1)
                if t:
                    pe.wait_ge(L.pt_act, TILES * i + t)
                    pe.wait_ge(L.pt_dve, TILES * i + t)
                for h in range(2):
                    for j in range(h * TILES // 2, (h + 1) * TILES // 2):
                        last = nc.tensor.transpose(pc[:, j * P:(j + 1) * P], probs[:, t % 2, j * P:(j + 1) * P], ident)
                    last.then_inc(L.pt_mm, 1)
                if t:
                    weigh_values(t - 1)
                if t + 2 < TILES:
                    scores(L, t + 2, q, k)
            pe.wait_ge(L.pt_act, TILES * i + TILES)
            pe.wait_ge(L.pt_dve, TILES * i + TILES)
            weigh_values(TILES - 1)
            for t in range(TILES):
                pe.wait_ge(L.o_norm, TILES * i + t + 1)
                last = nc.tensor.transpose(pa[:, t * P:(t + 1) * P], oT[:, t, :], ident)
            last.then_inc(L.ot_mm, 1)

        @block.tensor
        def _(pe):
            pe.wait_ge(weights0_in, 16)
            with pe.Fori(0, BATCH) as i:
                pe.wait_ge(cells_done, CORNERS * i)
                pe.wait_ge(x1_ready, i)
                pe.wait_ge(tab_copied, 3 * i)
                pe.wait_ge(off_read, i)
                pe_attention(pe, L0, i, xcur, wt("wq0"), wt("wk0"), wt("wv0"), q_stack, k_stack, R)
                pe.wait_ge(o_split, i + 1)
                for h in range(2):
                    last = nc.tensor.matmul(pb[:, h * HALF:(h + 1) * HALF], wp0_stack[:, :],
                                            o_stack[:, h * HALF:(h + 1) * HALF], start=True, stop=True)
                last.then_inc(wp_mm, 1)
                pe.wait_ge(x1_ready, i + 1)
                pe.wait_ge(weights_in, 16)
                for h in range(2):
                    last = nc.tensor.matmul(pa[:, h * HALF:(h + 1) * HALF], wt("w1"),
                                            xall[:, bass.ds(i, 1), h * HALF:(h + 1) * HALF].rearrange("p b n -> p (b n)"),
                                            start=True, stop=True)
                last.then_inc(conv1_mm, 1)
                pe.wait_ge(cells_done, CORNERS * i + CORNERS)
                for h in range(2):
                    for n, (a, b) in enumerate(((0, 0), (0, 1), (1, 0), (1, 1))):
                        last = nc.tensor.matmul(pb[n * R:(n + 1) * R, h * HALF:(h + 1) * HALF],
                                                wt("woff")[:, n * R:(n + 1) * R],
                                                cells[:, h * H // 2 + a:(h + 1) * H // 2 + a, b:b + W],
                                                start=True, stop=True)
                last.then_inc(off4_mm, 1)
                pe.wait_ge(off4_copied, i + 1)
                for t in range(TILES):
                    last = nc.tensor.matmul(pe_[:, t * OFFS:(t + 1) * OFFS], offs4[:, t * P:(t + 1) * P], wt("osum"),
                                            start=True, stop=True)
                last.then_inc(off_mm, 1)
                flat = cells[:, :, :].rearrange("p a b -> p (a b)")
                for k in range(TCHUNKS):
                    rows = P if k < TCHUNKS - 1 else TLAST
                    to = pc[0:rows, k * P:(k + 1) * P] if k < TILES else pd[0:rows, 0:P]
                    last = nc.tensor.transpose(to, flat[:, k * P:k * P + rows], ident)
                    if k in (3, 7, TCHUNKS - 1):
                        last.then_inc(tab_mm, 1)
            pe.wait_ge(tab_copied, 3 * BATCH)
            nc.tensor.matmul(pd[:, 0:C], wt("wvT3"), wt("wp3"), start=True, stop=True).then_inc(setup_pe, 1)
            pe.wait_ge(off_read, BATCH)
            nc.tensor.matmul(pe_[:, 0:C], wt("bv3"), wt("wp3"), start=True, stop=True).then_inc(setup_pe, 1)
            pe.wait_ge(setup_act, 2)
            with pe.Fori(0, BATCH) as i:
                pe.wait_ge(L3.o_norm, TILES * i)
                for t in range(TILES):
                    pe.wait_ge(sample_ready, TILES * i + t + 1)
                    if t >= 2:
                        pe.wait_ge(st_copied, TILES * i + t - 1)
                    for g in range(TURNS):
                        last = nc.tensor.transpose(single[t % 2][0:TR, g * P:(g + 1) * P],
                                                   samples[:, t % 2, g * TR:(g + 1) * TR], ident)
                    last.then_inc(st_mm, 1)
                pe.wait_ge(st_copied, TILES * i + TILES)
                for h in range(2):
                    for g in range(TURNS):
                        last = nc.tensor.matmul(pb[:, h * HALF:(h + 1) * HALF], wt("w2", TR)[:, g * P:(g + 1) * P],
                                                samplesT[:, g, h * HALF:(h + 1) * HALF],
                                                start=g == 0, stop=g == TURNS - 1)
                last.then_inc(w2_mm, 1)
                pe.wait_ge(h2_split, i + 1)
                pe.wait_ge(y_ready, i)
                for h in range(2):
                    last = nc.tensor.matmul(pa[:, h * HALF:(h + 1) * HALF], w3_stack[:, :],
                                            h2_stack[:, h * HALF:(h + 1) * HALF], start=True, stop=True)
                last.then_inc(w3_mm, 1)
                pe_attention(pe, L2, i, x2, wt("wq2"), wt("wk2"), wt("wv2"), q_stack, k_stack, C)
                pe.wait_ge(mom_ready, i + 1)
                nc.tensor.matmul(pd[:, 0:2], wt("gavg"), mom[:, :], start=True, stop=True).then_inc(g_mm, 1)
                pe_attention(pe, L3, i, h3, wt("wq3"), wt("wk3"), u3[:, :], q3, k3, C)

        def act_attention(act, L, i):
            def exponentials(t):
                act.wait_ge(L.max_done, TILES * i + t + 1)
                if t >= 2:
                    act.wait_ge(L.pt_mm, 2 * TILES * i + 2 * (t - 1))
                nc.scalar.activation(probs[:, t % 2, :], scores_bank[t % 2][:, :], ACT.Exp,
                                     bias=neg_max[:, t:t + 1], accum_out=denom[:, t:t + 1]).then_inc(L.exp_done, 1)

            exponentials(0)
            for t in range(TILES):
                if t + 1 < TILES:
                    exponentials(t + 1)
                act.wait_ge(L.pt_mm, 2 * TILES * i + 2 * t + 1)
                if t >= 2:
                    act.wait_ge(L.o_mm, TILES * i + t - 1)
                nc.scalar.activation(probsT[:, t % 2, 0:HALF], pc[:, 0:HALF], ACT.Copy).then_inc(L.pt_act, 1)

        @block.scalar
        def _(act):
            act.dma_start(xall[:, 0, :], x_view[0]).then_inc(x_in_sem[0], 16)
            act.dma_start(wts[:, FIRST:WIDTH], weights_dram[:, FIRST:WIDTH]).then_inc(weights_in, 16)
            act.wait_ge(weights_in, 16)
            act.wait_ge(setup_dve, 1)
            nc.scalar.activation(bn_std[:, :], bn_std[:, :], ACT.Sqrt).then_inc(setup_sqrt, 1)
            with act.Fori(0, BATCH) as i:
                act.wait_ge(L0.q_mm, i + 1)
                nc.scalar.activation(q_stack[:, :], pa[:, :], ACT.Copy, scale=float(R) ** -0.5).then_inc(L0.q_high, 1)
                act.wait_ge(L0.k_mm, i + 1)
                nc.scalar.activation(k_stack[:, :], pb[:, :], ACT.Copy).then_inc(L0.k_high, 1)
                act.wait_ge(L0.v_mm, i + 1)
                nc.scalar.activation(vT[:, :, 0:R], pc[:, 0:TILES * R].rearrange("p (j r) -> p j r", r=R),
                                     ACT.Copy).then_inc(L0.v_ready, 1)
                act_attention(act, L0, i)
                act.wait_ge(L0.ot_mm, i + 1)
                nc.scalar.activation(o_stack[:, :], pa[:, :], ACT.Copy).then_inc(o_high, 1)
                act.wait_ge(conv1_mm, i + 1)
                act.wait_ge(setup_dve, 2)
                for c in range(CORNERS):
                    dy, dx = c // 2, c % 2
                    at = slice(c * R, (c + 1) * R)
                    nc.scalar.activation(cells[at, 1 - dy:1 - dy + H, 1 - dx:1 - dx + W],
                                         pa[at, :].rearrange("p (a b) -> p a b", b=W), ACT.Relu,
                                         bias=bn_t[at, 0:1], scale=bn_s[at, 0:1]).then_inc(cells_done, 1)
                act.wait_ge(off4_mm, i + 1)
                nc.scalar.activation(offs4[:, :], pb[:, :], ACT.Identity, bias=wt("boff")).then_inc(off4_copied, 1)
                act.wait_ge(off_read, i + 1)
                nc.scalar.activation(mexp[:, :, :], offs[:, :, YX:OFFS], ACT.Exp, scale=-1.0).then_inc(mask_exp, 1)
                for k, (bank, a, b) in enumerate(((pc, 0, 4), (pc, 4, 8), (pd, 8, 9))):
                    rows = P if k < 2 else TLAST
                    act.wait_ge(tab_mm, 3 * i + k + 1)
                    base = 0 if k == 2 else a * P
                    nc.scalar.activation(tabS[0:rows, bass.ds(i, 1), a:b, :].rearrange("p i k d -> p (i k) d"),
                                         bank[0:rows, base:base + (b - a) * P].rearrange("p (k d) -> p k d", d=P),
                                         ACT.Copy).then_inc(tab_copied, 1)
            for n, (to, bank) in enumerate(((u3, pd), (bvp3, pe_))):
                act.wait_ge(setup_pe, n + 1)
                nc.scalar.activation(to[:, :], bank[:, 0:C], ACT.Copy).then_inc(setup_act, 1)
            with act.Fori(0, BATCH) as i:
                for t in range(TILES):
                    act.wait_ge(st_mm, TILES * i + t + 1)
                    nc.scalar.activation(samplesT[:, :, t * P:(t + 1) * P],
                                         single[t % 2][0:TR, 0:TURNS * P].rearrange("p (g n) -> p g n", g=TURNS),
                                         ACT.Copy).then_inc(st_copied, 1)
                act.wait_ge(w2_mm, i + 1)
                nc.scalar.activation(h2_full[:, :], pb[:, :], ACT.Relu, bias=bn_t[:, 1:2], scale=bn_s[:, 1:2]).then_inc(h2_high, 1)
                nc.scalar.activation(h2_stack[:, :], pb[:, :], ACT.Relu, bias=bn_t[:, 1:2],
                                     scale=bn_s[:, 1:2]).then_inc(h2_high, 1)
                act.wait_ge(x2_added, i + 1)
                nc.scalar.activation(x2[:, :], x2_sum[:, :], ACT.Relu, bias=bn_t[:, 2:3]).then_inc(L2.x_ready, 1)
                act.wait_ge(L2.q_mm, i + 1)
                nc.scalar.activation(q_stack[:, :], pa[:, :], ACT.Identity, bias=wt("bq2")).then_inc(L2.q_high, 1)
                act.wait_ge(L2.k_mm, i + 1)
                nc.scalar.activation(k_stack[:, :], pb[:, :], ACT.Identity, bias=wt("bk2")).then_inc(L2.k_high, 1)
                act_attention(act, L2, i)
                act.wait_ge(gvar_ready, i + 1)
                nc.scalar.activation(gstd[:, :], gvar[:, :], ACT.Sqrt).then_inc(gstd_ready, 1)
                act.wait_ge(gaff_ready, i + 1)
                nc.scalar.activation(h3[:, :], x3[:, :], ACT.Identity, bias=gbias[:, :], scale=gscale[:, :]).then_inc(L3.x_ready, 1)
                act.wait_ge(L3.q_mm, i + 1)
                nc.scalar.activation(q3[:, :], pa[:, :], ACT.Identity, bias=bq3s[:, :], scale=float(C) ** -0.5).then_inc(L3.q_ready, 1)
                act.wait_ge(L3.k_mm, i + 1)
                nc.scalar.activation(k3[:, :], pb[:, :], ACT.Identity, bias=wt("bk3")).then_inc(L3.k_ready, 1)
                act_attention(act, L3, i)
                nc.scalar.activation(x3s[:, :], x3[:, :], ACT.Identity, bias=bp3s[:, :], scale=2.0 ** -0.5).then_inc(x3s_ready, 1)

        def dve_attention(dve, L, i, width):
            copies = C // width

            def maximum(t):
                dve.wait_ge(L.s_mm, TILES * i + t + 1)
                nc.vector.tensor_reduce(neg_max[:, t:t + 1], scores_bank[t % 2][:, :], axis=X, op=ALU.max,
                                        negate=True).then_inc(L.max_done, 1)

            def normalise(t):
                dve.wait_ge(L.o_mm, TILES * i + t + 1)
                dve.wait_ge(L.inv_done, TILES * i + t + 1)
                src = single[t % 2][:, 0:width]
                dst = oT[:, t, :]
                if copies > 1:
                    src = src.rearrange("p (a r) -> p a r", a=1).to_broadcast([P, copies, width])
                    dst = dst.rearrange("p (a r) -> p a r", a=copies)
                nc.vector.tensor_scalar(dst, src, inv_denom[:, t:t + 1], None, ALU.mult).then_inc(L.o_norm, 1)

            maximum(0)
            for t in range(TILES):
                if t + 1 < TILES:
                    maximum(t + 1)
                dve.wait_ge(L.exp_done, TILES * i + t + 1)
                nc.vector.reciprocal(inv_denom[:, t:t + 1], denom[:, t:t + 1]).then_inc(L.inv_done, 1)
                dve.wait_ge(L.pt_mm, 2 * TILES * i + 2 * t + 2)
                if t >= 2:
                    dve.wait_ge(L.o_mm, TILES * i + t - 1)
                nc.vector.tensor_copy(probsT[:, t % 2, HALF:N], pc[:, HALF:N]).then_inc(L.pt_dve, 1)
                if t:
                    normalise(t - 1)
            normalise(TILES - 1)

        def both(t):
            return t[:, :, :].rearrange("p t (a k) -> p t a k", a=2)

        @block.vector
        def _(dve):
            nc.vector.memset(cells[:, :, :], 0.0)
            dve.sem_inc(slot_free, TILES)
            dve.wait_ge(weights0_in, 16)
            nc.vector.tensor_copy(wp0_stack[:, :], wt("wp0"))
            dve.drain()
            for c in (1, 3):
                at = slice(c * R, (c + 1) * R)
                nc.vector.tensor_tensor(wp0_stack[at, :], wt("wp0")[at, :], wp0_stack[at, :].bitcast(fp32), ALU.subtract)
            dve.wait_ge(x_in_sem[0], 16)
            nc.vector.tensor_copy(xcur[:, :], xall[:, 0, :]).then_inc(L0.x_ready, 1)
            dve.wait_ge(weights_in, 16)
            nc.vector.tensor_scalar(bn_std[:, :], wt("bn_v"), EPS, None, ALU.add).then_inc(setup_dve, 1)
            nc.vector.tensor_copy(w3_stack[:, :], wt("w3"))
            nc.vector.tensor_scalar(bq3s[:, :], wt("bq3"), float(C) ** -0.5, None, ALU.mult)
            nc.vector.tensor_scalar(bp3s[:, :], wt("bp3"), 2.0 ** -0.5, None, ALU.mult)
            dve.drain()
            for c in (1, 3):
                at = slice(c * R, (c + 1) * R)
                nc.vector.tensor_tensor(w3_stack[at, :], wt("w3")[at, :], w3_stack[at, :].bitcast(fp32), ALU.subtract)
            dve.wait_ge(setup_sqrt, 1)
            nc.vector.reciprocal(bn_s[:, :], bn_std[:, :])
            dve.drain()
            nc.vector.tensor_tensor(bn_s[:, :], bn_s[:, :], wt("bn_g"), ALU.mult)
            dve.drain()
            nc.vector.tensor_tensor(bn_t[:, :], wt("bn_m"), bn_s[:, :], ALU.mult)
            dve.drain()
            nc.vector.tensor_tensor(bn_t[:, :], wt("bn_b"), bn_t[:, :], ALU.subtract)
            dve.drain()
            nc.vector.scalar_tensor_tensor(bn_t[:, 1:2], bn_s[:, 1:2], wt("dcn_b"), bn_t[:, 1:2], ALU.mult,
                                           ALU.add).then_inc(setup_dve, 1)
            for b in range(1, BATCH):
                dve.wait_ge(x_in_sem[b], 16)

            with dve.Fori(0, BATCH) as i:
                dve.wait_ge(L0.q_high, i + 1)
                nc.vector.scalar_tensor_tensor(q_stack[2 * R:4 * R, :], pa[2 * R:4 * R, :], float(R) ** -0.5,
                                               q_stack[2 * R:4 * R, :].bitcast(fp32), ALU.mult,
                                               ALU.subtract).then_inc(L0.q_ready, 1)
                dve.wait_ge(L0.k_high, i + 1)
                for c in (1, 3):
                    at = slice(c * R, (c + 1) * R)
                    last = nc.vector.tensor_tensor(k_stack[at, :], pb[at, :], k_stack[at, :].bitcast(fp32), ALU.subtract)
                last.then_inc(L0.k_ready, 1)
                dve_attention(dve, L0, i, R)
                dve.wait_ge(o_high, i + 1)
                nc.vector.tensor_tensor(o_stack[2 * R:4 * R, :], pa[2 * R:4 * R, :],
                                        o_stack[2 * R:4 * R, :].bitcast(fp32), ALU.subtract).then_inc(o_split, 1)
                dve.wait_ge(wp_mm, i + 1)
                here = xall[:, bass.ds(i, 1), :].rearrange("p b n -> p (b n)")
                nc.vector.tensor_tensor(here, pb[:, :], xcur[:, :], ALU.add).then_inc(x1_ready, 1)
                dve.drain()
                nc.vector.tensor_copy(xcur[:, :], xall[:, bass.ds((i + 1) & 3, 1), :].rearrange("p b n -> p (b n)"))\
                    .then_inc(L0.x_ready, 1)
                dve.wait_ge(off_mm, i + 1)
                nc.vector.tensor_copy(offs[:, :, :], pe_[:, 0:TILES * OFFS].rearrange("p (t k) -> p t k", k=OFFS))\
                    .then_inc(off_read, 1)
                dve.drain()
                nc.vector.tensor_tensor(yx[:, :, :], offs[:, :, 0:YX],
                                        wt("base").rearrange("p (t k) -> p t k", k=YX), ALU.add)
                dve.drain()
                nc.vector.tensor_scalar(yx[:, :, :], yx[:, :, :], -1.0, float(H), ALU.max, ALU.min)
                dve.drain()
                nc.vector.tensor_scalar(low[:, :, :], yx[:, :, :], 0.5, ROUND, ALU.add, ALU.add)
                dve.drain()
                nc.vector.tensor_scalar(low[:, :, :], low[:, :, :], ROUND, None, ALU.subtract)
                dve.drain()
                nc.vector.scalar_tensor_tensor(rows_all[:, bass.ds(i, 1), :].rearrange("p b (t k) -> p (b t) k", k=TAPS),
                                               low[:, :, 0:TAPS], float(CELLS), low[:, :, TAPS:YX],
                                               ALU.mult, ALU.add).then_inc(rows_ready, 1)
                nc.vector.scalar_tensor_tensor(frac[:, :, :], yx[:, :, :], 1.0, low[:, :, :], ALU.add, ALU.subtract)
                dve.drain()
                nc.vector.tensor_scalar(rest[:, :, :], frac[:, :, :], -1.0, 1.0, ALU.mult, ALU.add)
                dve.wait_ge(mask_exp, i + 1)
                nc.vector.tensor_scalar(mask[:, :, :], mexp[:, :, :], 1.0, None, ALU.add)
                dve.drain()
                nc.vector.reciprocal(mask[:, :, :], mask[:, :, :])
                dve.drain()
                for dy, part in enumerate((rest, frac)):
                    nc.vector.tensor_tensor(wy[:, dy, :, :], part[:, :, 0:TAPS], mask[:, :, :], ALU.mult)
                dve.drain()
                for c in range(CORNERS):
                    part = (rest, frac)[c % 2]
                    to = corner_w[:, bass.ds(i, 1), :, :].rearrange("p b t (k c) -> p (b t k) c", c=CORNERS)[:, :, c]
                    last = nc.vector.tensor_tensor(to.rearrange("p (t k) -> p t k", k=TAPS), wy[:, c // 2, :, :],
                                                   part[:, :, TAPS:YX], ALU.mult)
                last.then_inc(corner_ready, 1)

            dve.wait_ge(corner_ready, BATCH)
            with dve.Fori(0, BATCH) as i:
                for t in range(TILES):
                    dve.wait_ge(got_sem[t], 16 * TAPS * (i + 1))
                    w = corner_w[:, bass.ds(i, 1), t, :].rearrange("p b k -> p (b k)")
                    nc.vector.tensor_tensor(weighed[:, t % 2, :, :].rearrange("p k (c r) -> p (k c) r", r=R),
                                            got[:, t, :, :].rearrange("p k (c r) -> p (k c) r", r=R),
                                            w.rearrange("p (k a) -> p k a", a=1).to_broadcast([P, TAPS * CORNERS, R]),
                                            ALU.mult).then_inc(slot_free, 1)
                    dve.drain()
                    if t >= 2:
                        dve.wait_ge(st_mm, TILES * i + t - 1)
                    nc.vector.tensor_reduce(samples[:, t % 2, :].rearrange("p (k r) -> p k r", r=R),
                                            weighed[:, t % 2, :, :].rearrange("p k (c r) -> p k r c", r=R),
                                            axis=X, op=ALU.add).then_inc(sample_ready, 1)
                dve.wait_ge(h2_high, 2 * i + 2)
                nc.vector.tensor_tensor(h2_stack[2 * R:4 * R, :], h2_full[2 * R:4 * R, :],
                                        h2_stack[2 * R:4 * R, :].bitcast(fp32), ALU.subtract).then_inc(h2_split, 1)
                dve.wait_ge(w3_mm, i + 1)
                nc.vector.scalar_tensor_tensor(x2_sum[:, :], pa[:, :], bn_s[:, 2:3],
                                               xall[:, bass.ds(i, 1), :].rearrange("p b n -> p (b n)"),
                                               ALU.mult, ALU.add).then_inc(x2_added, 1)

                dve.wait_ge(L2.q_high, i + 1)
                nc.vector.scalar_tensor_tensor(q_stack[2 * R:4 * R, :], pa[2 * R:4 * R, :], wt("bq2")[2 * R:4 * R, :],
                                               q_stack[2 * R:4 * R, :].bitcast(fp32), ALU.add,
                                               ALU.subtract).then_inc(L2.q_ready, 1)
                dve.wait_ge(L2.k_high, i + 1)
                for c in (1, 3):
                    at = slice(c * R, (c + 1) * R)
                    last = nc.vector.scalar_tensor_tensor(k_stack[at, :], pb[at, :], wt("bk2")[at, :],
                                                          k_stack[at, :].bitcast(fp32), ALU.add, ALU.subtract)
                last.then_inc(L2.k_ready, 1)
                dve.wait_ge(L2.v_mm, i + 1)
                nc.vector.tensor_tensor(vT[:, :, :], pc[:, :].rearrange("p (j c) -> p j c", c=C),
                                        wt("bv2").rearrange("p (a c) -> p a c", a=1).to_broadcast([P, TILES, C]),
                                        ALU.add).then_inc(L2.v_ready, 1)
                dve_attention(dve, L2, i, C)
                dve.wait_ge(L2.ot_mm, i + 1)
                nc.vector.scalar_tensor_tensor(x3[:, :], pa[:, :], wt("gamma"), x2[:, :], ALU.mult, ALU.add)
                dve.drain()

                for h in range(2):
                    nc.vector.bn_stats(stats[:, h, :], x3[:, h * HALF:(h + 1) * HALF])
                dve.drain()
                nc.vector.bn_aggr(mom[:, :], stats[:, :, :].rearrange("p h s -> p (h s)"))
                dve.drain()
                nc.vector.scalar_tensor_tensor(mom[:, 1:2], mom[:, 0:1], mom[:, 0:1], mom[:, 1:2], ALU.mult,
                                               ALU.add).then_inc(mom_ready, 1)
                dve.wait_ge(g_mm, i + 1)
                nc.vector.tensor_copy(gmom[:, :], pd[:, 0:2])
                dve.drain()
                nc.vector.tensor_scalar(gsq[:, :], gmom[:, 0:1], gmom[:, 0:1], EPS, ALU.mult, ALU.subtract)
                dve.drain()
                nc.vector.tensor_tensor(gvar[:, :], gmom[:, 1:2], gsq[:, :], ALU.subtract).then_inc(gvar_ready, 1)
                dve.wait_ge(gstd_ready, i + 1)
                nc.vector.reciprocal(gscale[:, :], gstd[:, :])
                dve.drain()
                nc.vector.tensor_tensor(gscale[:, :], gscale[:, :], wt("gn_w"), ALU.mult)
                dve.drain()
                nc.vector.tensor_tensor(gbias[:, :], gmom[:, 0:1], gscale[:, :], ALU.mult)
                dve.drain()
                nc.vector.tensor_tensor(gbias[:, :], wt("gn_b"), gbias[:, :], ALU.subtract).then_inc(gaff_ready, 1)
                dve.wait_ge(L3.v_mm, i + 1)
                nc.vector.tensor_tensor(vT[:, :, :], pc[:, :].rearrange("p (j c) -> p j c", c=C),
                                        bvp3[:, :].rearrange("p (a c) -> p a c", a=1).to_broadcast([P, TILES, C]),
                                        ALU.add).then_inc(L3.v_ready, 1)
                dve_attention(dve, L3, i, C)
                dve.wait_ge(L3.ot_mm, i + 1)
                dve.wait_ge(x3s_ready, i + 1)
                dve.wait_ge(y_out, 16 * i)
                nc.vector.scalar_tensor_tensor(y[:, :], pa[:, :], 2.0 ** -0.5, x3s[:, :], ALU.mult,
                                               ALU.add).then_inc(y_ready, 1)


def pack(a):
    w = np.zeros((P, WIDTH), np.float32)

    def put(name, value):
        value = np.asarray(value, np.float32)
        value = value.reshape(value.shape[0], -1)
        w[:value.shape[0], AT[name][0]:AT[name][1]] = value

    def column(v):
        return np.asarray(v).reshape(-1, 1)

    four = lambda v: np.concatenate([v] * 4, axis=0)
    put("ident", np.eye(P))
    put("wq0", four(a["L0_conv_Wq"]).T)
    put("wk0", four(a["L0_conv_Wk"]).T)
    put("wv0", a["L0_conv_Wv"].T)
    put("wp0", four(a["L0_conv_Wp"].T))
    put("w1", four(a["L1_conv_w1"]).T)
    for n, (name, k) in enumerate((("bn_g", "g"), ("bn_b", "b"), ("bn_m", "m"), ("bn_v", "v"))):
        put(name, np.concatenate([column(four(a[f"L1_conv_bn1_{k}"])), column(four(a[f"L1_conv_bn2_{k}"])),
                                  column(a[f"L1_conv_bn3_{k}"])], axis=1))
    put("dcn_b", column(four(a["L1_conv_dcn_b"])))
    order = [2 * k for k in range(TAPS)] + [2 * k + 1 for k in range(TAPS)] + list(range(YX, OFFS))
    woff = a["L1_conv_woff"][order]
    to = np.zeros((CORNERS, R, 4, R), np.float32)
    for n, (oy, ox) in enumerate(((0, 0), (0, 1), (1, 0), (1, 1))):
        for c in range(CORNERS):
            ky, kx = oy + c // 2, ox + c % 2
            if (oy == 0 or ky == 2) and (ox == 0 or kx == 2):
                to[c, :, n, :OFFS] = woff[:, :, ky, kx].T
    put("woff", to.reshape(P, -1))
    put("boff", column(a["L1_conv_boff"][order]))
    put("osum", np.concatenate([np.eye(R, OFFS)] * 4, axis=0))
    p, t, k = np.arange(P)[:, None, None], np.arange(TILES)[None, :, None], np.arange(TAPS)[None, None, :]
    by, bx = t * ROWS + p // W - 1 + k // 3, p % W - 1 + k % 3 + 0 * t
    put("base", np.concatenate([by, bx], axis=2))
    w2 = a["L1_conv_w2"].reshape(R, R, TURNS, TAPS_A_TURN).transpose(3, 1, 2, 0)
    put("w2", np.concatenate([w2] * 4, axis=3).reshape(TR, TURNS * P))
    put("w3", four(a["L1_conv_w3"].T))
    pad = lambda v: four(np.concatenate([v, np.zeros((R - QK2,) + v.shape[1:], np.float32)], axis=0))
    put("wq2", pad(a["L2_conv_wq"]).T)
    put("wk2", pad(a["L2_conv_wk"]).T)
    put("wv2", a["L2_conv_wv"].T)
    put("bq2", column(pad(a["L2_conv_bq"])))
    put("bk2", column(pad(a["L2_conv_bk"])))
    put("bv2", np.broadcast_to(a["L2_conv_bv"], (P, C)))
    put("gamma", column(a["L2_conv_gamma"]))
    put("wq3", a["L3_conv_Wq"])
    put("wk3", a["L3_conv_Wk"])
    put("wvT3", a["L3_conv_Wv"].T)
    put("wp3", a["L3_conv_Wp"])
    for k in ("bq", "bk", "bp"):
        put(k + "3", column(a["L3_conv_" + k]))
    put("bv3", np.broadcast_to(column(a["L3_conv_bv"]), (C, P)))
    put("gn_w", column(a["L3_conv_gn_w"]))
    put("gn_b", column(a["L3_conv_gn_b"]))
    put("gavg", np.kron(np.eye(C // GROUP), np.full((GROUP, GROUP), 1.0 / GROUP)))
    return w


def kernel(**inputs):
    import concourse.bacc as bacc
    from concourse.bass_utils import run_bass_kernel_spmd

    a = {k: np.asarray(v) for k, v in inputs.items()}
    x, w = np.ascontiguousarray(a["x"]), pack(a)
    nc = bacc.Bacc("TRN2", target_bir_lowering=False, num_devices=1)
    fp32 = mybir.dt.float32
    x_ap = nc.dram_tensor("x_dram", x.shape, fp32, kind="ExternalInput").ap()
    w_ap = nc.dram_tensor("weights_dram", w.shape, fp32, kind="ExternalInput").ap()
    o_ap = nc.dram_tensor("out_dram", x.shape, fp32, kind="ExternalOutput").ap()
    build(nc, x_ap, w_ap, o_ap)
    result = run_bass_kernel_spmd(nc, [{"x_dram": x, "weights_dram": w}], core_ids=[0])
    return result.results[0]["out_dram"]
```

```python
import numpy as np
import concourse.bass as bass
from concourse import mybir
from contextlib import ExitStack

BATCH, C, H, W = 4, 128, 32, 32
N = H * W
P = 128
TILES = N // P
ROWS = P // W
HALF = 512
R = 32
QK2 = C // 8
TAPS = 9
CORNERS = 4
GROUP = C // 32
EPS = 1e-5
CELLS = H + 1
TABLE = CELLS * CELLS
TCHUNKS = -(-TABLE // P)
TLAST = TABLE - (TCHUNKS - 1) * P
YX = 2 * TAPS
OFFS = 3 * TAPS
TAPS_A_TURN = 3
TURNS = TAPS // TAPS_A_TURN
TR = TAPS_A_TURN * R
ROUND = 1.5 * 2 ** 23

PLACES = ((0, 0), (0, 1), (1, 0), (1, 1))
COLUMNS = [
    ("ident", P), ("wq0", P), ("wk0", P), ("wv0", R), ("wp0", P), ("ones", 1),
    ("ones0", R), ("dsum", 1),
    ("w1", P), ("bn_g", 3), ("bn_b", 3), ("bn_m", 3), ("bn_v", 3), ("dcn_b", 1),
    ("woff", 4 * R), ("boff", 1), ("osum", OFFS), ("base", TILES * YX), ("w2", TURNS * P), ("w3", P),
    ("wq2", P), ("wk2", P), ("wv2", C), ("bq2", 1), ("bk2", 1), ("bv2", C), ("gamma", 1),
    ("wq3", C), ("wk3", C), ("wvT3", C), ("wp3", C), ("bq3", 1), ("bk3", 1), ("bv3", P), ("bp3", 1),
    ("gn_w", 1), ("gn_b", 1), ("gavg", P),
]
AT, _at = {}, 0
for _name, _width in COLUMNS:
    AT[_name] = (_at, _at + _width)
    _at += _width
WIDTH = _at
FIRST = AT["w1"][0]


def build(nc, x_dram, weights_dram, out_dram):
    fp32, fp32r, bf16, int32 = mybir.dt.float32, mybir.dt.float32r, mybir.dt.bfloat16, mybir.dt.int32
    ALU, ACT, X = mybir.AluOpType, mybir.ActivationFunctionType, mybir.AxisListType.X
    x_view = x_dram.rearrange("b c h w -> b c (h w)")
    out_view = out_dram.rearrange("b c h w -> b c (h w)")
    ctx = ExitStack()
    with ctx:
        def sb(name, shape, dt=fp32):
            return ctx.enter_context(nc.sbuf_tensor(name, shape, dt))

        def sem(name):
            return ctx.enter_context(nc.semaphore(name))

        tables = [nc.dram_tensor(f"cell_table{n}", (TABLE, CORNERS * R), fp32).ap() for n in range(2)]

        wts = sb("wts", [P, WIDTH])

        def wt(name, rows=P):
            a, b = AT[name]
            return wts[0:rows, a:b]

        ident = wt("ident")
        xall = sb("xall", [P, BATCH, N])
        xcur = x2 = sb("xcur_x2", [P, N])
        x3 = sb("x3", [P, N])
        h3 = sb("h3", [P, N])
        q_stack = sb("q_stack", [P, N], fp32r)
        k_stack = sb("k_stack", [P, N], fp32r)
        ident16 = sb("ident16", [P, P], bf16)
        neg_max = sb("neg_max", [P, TILES])
        shift = sb("shift", [P, TILES, R], bf16)
        vT = sb("vT", [P, TILES, C + 1])
        expT = sb("expT", [P, TILES, N])
        inv = sb("inv", [P, TILES])
        oT = sb("oT", [P, TILES, C])
        o4 = oT[:, :, :].rearrange("p t c -> p (t c)")
        h2_stack = sb("h2_stack", [P, N], fp32r)
        w3_stack = sb("w3_stack", [P, P], fp32r)
        bn_std = sb("bn_std", [P, 3])
        bn_s = sb("bn_s", [P, 3])
        bn_t = sb("bn_t", [P, 3])
        cells = sb("cells", [P, CELLS, CELLS])
        tabS = sb("tabS", [P, BATCH, TCHUNKS, P])
        x3s = y = cells[:, :, :].rearrange("p a b -> p (a b)")[:, 0:N]
        offs4 = h2_full = x2_sum = sb("offs4_h2_full_x2_sum", [P, N])
        probsT = sb("probsT", [P, N])
        at = 0
        coordinates = []
        for width in (OFFS, YX, YX, YX, YX, TAPS, TAPS):
            coordinates.append(probsT[:, at:at + TILES * width].rearrange("p (t k) -> p t k", k=width))
            at += TILES * width
        offs, yx, low, frac, rest, mask, mexp = coordinates
        wy = sb("wy", [P, 2, TILES, TAPS])
        rows_all = sb("rows_all", [P, BATCH, TILES * TAPS], int32)
        rows_cur = sb("rows_cur", [P, 2, TILES * TAPS], int32)
        corner_w = sb("corner_w", [P, BATCH, TILES, TAPS * CORNERS])
        got = sb("got", [P, TILES, TAPS, CORNERS * R])
        weighed = sb("weighed", [P, TAPS, CORNERS * R])
        samples = sb("samples", [P, 2, TAPS * R])
        samplesT = sb("samplesT", [TR, TURNS, N])
        stats = sb("stats", [P, 2, 6])
        mom = sb("mom", [P, 2])
        gmom = sb("gmom", [P, 2])
        gsq = sb("gsq", [P, 1])
        gvar = sb("gvar", [P, 1])
        gstd = sb("gstd", [P, 1])
        gscale = sb("gscale", [P, 1])
        gbias = sb("gbias", [P, 1])
        q3 = sb("q3", [P, N])
        k3 = sb("k3", [P, N])
        v3T = sb("v3T", [P, TILES, C])
        u3 = sb("u3", [P, C])
        bvp3 = sb("bvp3", [P, C])
        bq3s = sb("bq3s", [P, 1])
        bp3s = sb("bp3s", [P, 1])
        neg_max3 = sb("neg_max3", [P, TILES])
        denom3 = sb("denom3", [P, TILES])
        inv3 = sb("inv3", [P, TILES])
        probs = sb("probs", [P, 2, N])
        d4, inv0 = probs[:, 0, :], probs[:, 1, :]
        o3T = h3[:, :].rearrange("p (t c) -> p t c", c=C)

        def pb(name, width):
            return ctx.enter_context(nc.psum_tensor(name, [P, width], fp32))

        xs, xq, ys, yy = pb("xs", N), pb("xq", N), pb("ys", N), pb("yy", N)
        xo, xp = xq[:, 0:HALF], xq[:, HALF:N]
        yo, yt = yy[:, 0:HALF], yy[:, HALF:N]

        weights0_in = sem("weights0_in")
        weights_in = sem("weights_in")
        x_in = [sem(f"x_in{b}") for b in range(BATCH)]
        setup_dve = sem("setup_dve")
        setup_sqrt = sem("setup_sqrt")
        setup_pe = sem("setup_pe")
        setup_act = sem("setup_act")
        x_ready, q_mm, q_high, q_ready, k_mm, k_high, k_ready, v_mm, v_ready = ({
            n: sem(f"{what}_{n}") for n in (0, 2)} for what in (
            "x_ready",
            "q_mm", "q_high", "q_ready",
            "k_mm", "k_high", "k_ready",
            "v_mm", "v_ready"))
        s_mm, max_done, shift_ready, shift_mm, shift_done, t_mm, exp_done, o_mm = ({
            n: sem(f"{what}_{n}") for n in (0, 2)} for what in (
            "s_mm", "max_done",
            "shift_ready", "shift_mm", "shift_done",
            "t_mm", "exp_done",
            "o_mm"))
        o_norm = sem("o_norm")
        ot_mm = sem("ot_mm")
        d4_mm, d4_copied = sem("d4_mm"), sem("d4_copied")
        o4_copied = sem("o4_copied")
        d_mm = sem("d_mm")
        inv0_done = sem("inv0_done")
        inv0_mm = sem("inv0_mm")
        wp_mm = sem("wp_mm")
        x1_ready = sem("x1_ready")
        conv1_mm = sem("conv1_mm")
        cells_done = sem("cells_done")
        off4_mm = sem("off4_mm")
        off4_copied = sem("off4_copied")
        off_mm = sem("off_mm")
        off_read = sem("off_read")
        mask_exp = sem("mask_exp")
        rows_ready = sem("rows_ready")
        corner_ready = sem("corner_ready")
        tab_mm = sem("tab_mm")
        tab_copied = sem("tab_copied")
        tab_out = [sem(f"tab_out{n}") for n in range(2)]
        table_free = sem("table_free")
        rows_copied = sem("rows_copied")
        sp_go, pool_go = sem("sp_go"), sem("pool_go")
        got_sem = [sem(f"got{t}") for t in range(TILES)]
        slot_free = sem("slot_free")
        sample_ready = sem("sample_ready")
        st_mm = sem("st_mm")
        st_copied = sem("st_copied")
        w2_mm = sem("w2_mm")
        h2_high = sem("h2_high")
        h2_split = sem("h2_split")
        w3_mm = sem("w3_mm")
        x2_added = sem("x2_added")
        x3_ready = sem("x3_ready")
        mom_ready = sem("mom_ready")
        g_mm = sem("g_mm")
        gvar_ready = sem("gvar_ready")
        gstd_ready = sem("gstd_ready")
        gaff_ready = sem("gaff_ready")
        h3_ready = sem("h3_ready")
        q3_mm = sem("q3_mm")
        q3_ready = sem("q3_ready")
        k3_mm = sem("k3_mm")
        k3_ready = sem("k3_ready")
        v3_mm = sem("v3_mm")
        v3_ready = sem("v3_ready")
        s3_mm = sem("s3_mm")
        max3_done = sem("max3_done")
        exp3_done = sem("exp3_done")
        inv3_done = sem("inv3_done")
        pt_mm = sem("pt_mm")
        pt_act = sem("pt_act")
        pt_dve = sem("pt_dve")
        o3_mm = sem("o3_mm")
        o3_norm = sem("o3_norm")
        ot3_mm = sem("ot3_mm")
        y_ready = sem("y_ready")
        y_out = sem("y_out")

        block = ctx.enter_context(nc.Block())

        def halves(bank):
            return [(bank[:, h * HALF:(h + 1) * HALF], slice(h * HALF, (h + 1) * HALF)) for h in range(2)]

        def quarter(c, n=1):
            return slice(c * R, (c + n) * R)

        @block.sync
        def _(sp):
            sp.dma_start(wts[:, 0:FIRST], weights_dram[:, 0:FIRST]).then_inc(weights0_in, 16)
            for b in range(1, BATCH):
                sp.dma_start(xall[:, b, :], x_view[b]).then_inc(x_in[b], 16)
            tab_pair = tabS[:, :, :, :].rearrange("p (a n) k d -> p a n k d", n=2)
            with sp.Fori(0, BATCH // 2) as i:
                for n, table in enumerate(tables):
                    sp.wait_ge(tab_copied, 6 * i + 3 * n + 3)
                    sp.sem_inc(sp_go, 1)
                    sp.wait_ge(table_free, 2 * i + n + 1)
                    sp.sem_inc(sp_go, 1)
                    sp.dma_start(table[0:(TCHUNKS - 1) * P, :].rearrange("(k p) d -> p k d", p=P),
                                 tab_pair[:, bass.ds(i, 1), n, 0:TCHUNKS - 1, :].rearrange("p a k d -> p (a k) d"))\
                        .then_inc(tab_out[n], 16)
                    sp.dma_start(table[(TCHUNKS - 1) * P:TABLE, :],
                                 tab_pair[0:TLAST, bass.ds(i, 1), n, TCHUNKS - 1, :].rearrange("p a d -> p (a d)"))\
                        .then_inc(tab_out[n], 16)
            with sp.Fori(0, BATCH) as i:
                sp.wait_ge(y_ready, i + 2)
                sp.sem_inc(sp_go, 1)
                sp.dma_start(out_view[bass.ds(i, 1), :, :].rearrange("b c n -> (b c) n"), y[:, :]).then_inc(y_out, 16)
            sp.wait_ge(y_out, 16 * BATCH + 16)
            for n in range(2):
                sp.wait_ge(tab_out[n], 16 * BATCH)

        @block.gpsimd
        def _(pool):
            rows_pair = rows_all[:, :, :].rearrange("p (a n) k -> p a n k", n=2)
            with pool.Fori(0, BATCH // 2) as i:
                for n, table in enumerate(tables):
                    pool.wait_ge(rows_ready, 2 * i + n + 1)
                    nc.gpsimd.tensor_copy(rows_cur[:, n, :], rows_pair[:, bass.ds(i, 1), n, :].rearrange("p a k -> p (a k)"))\
                        .then_inc(rows_copied, 1)
                    pool.wait_ge(rows_copied, 2 * i + n + 1)
                    pool.wait_ge(tab_out[n], 32 * i + 32)
                    for t in range(TILES):
                        pool.wait_ge(slot_free, 2 * TILES * i + TILES * n + t + 1)
                        pool.sem_inc(pool_go, 1)
                        for k in range(TAPS):
                            at = t * TAPS + k
                            nc.gpsimd.indirect_dma_start(
                                got[:, t, k, :], None, table,
                                bass.IndirectOffsetOnAxis(ap=rows_cur[:, n, at:at + 1], axis=0)).then_inc(got_sem[t], 16)

        @block.tensor
        def _(pe):
            def project(to, w, x, done):
                for bank, at in halves(to):
                    last = nc.tensor.matmul(bank, w, x[:, at], start=True, stop=True)
                last.then_inc(done, 1)

            def scores(L, i, t, bank):
                for to, at in halves(bank):
                    last = nc.tensor.matmul(to, q_stack[0:3 * R, t * P:(t + 1) * P], k_stack[0:3 * R, at],
                                            start=True, stop=True)
                last.then_inc(s_mm[L], 1)

            def shift_rows(L, i, bank):
                pe.wait_ge(shift_ready[L], i + 1)
                for t in range(TILES):
                    last = nc.tensor.matmul(bank[3 * R:4 * R, t * P:(t + 1) * P], shift[:, t, :], ident16[:, :],
                                            start=True, stop=True)
                last.then_inc(shift_mm[L], 1)

            def shifted_scores(L, i, j, bank):
                for to, at in halves(bank):
                    last = nc.tensor.matmul(to, k_stack[:, j * P:(j + 1) * P], q_stack[:, at], start=True, stop=True)
                last.then_inc(t_mm[L], 1)

            def weigh_values(L, t, to, width):
                for j in range(TILES):
                    last = nc.tensor.matmul(to, expT[:, j, t * P:(t + 1) * P], vT[:, j, C - width:C + 1],
                                            start=j == 0, stop=j == TILES - 1)
                last.then_inc(o_mm[L], 1)

            def l0_project(i):
                pe.wait_ge(x_ready[0], i + 1)
                project(xq, wt("wq0"), xcur, q_mm[0])
                project(yy, wt("wk0"), xcur, k_mm[0])

            def l0_values_in(i, h):
                for j in range(h * TILES // 2, (h + 1) * TILES // 2):
                    last = nc.tensor.matmul(xo[:, j * R:(j + 1) * R], xcur[:, j * P:(j + 1) * P], wt("wv0"),
                                            start=True, stop=True)
                if h:
                    last.then_inc(v_mm[0], 1)

            def l0_scores(i, t):
                if t == 0:
                    pe.wait_ge(q_ready[0], i + 1)
                    pe.wait_ge(k_ready[0], i + 1)
                if t >= 2:
                    pe.wait_ge(max_done[0], TILES * i + t - 1)
                scores(0, i, t, (xs, ys)[t % 2])

            def l0_shift(i):
                pe.wait_ge(max_done[0], TILES * i + TILES - 1)
                shift_rows(0, i, xs)

            def l0_shifted(i, j):
                if j == 0:
                    pe.wait_ge(shift_done[0], i + 1)
                    pe.wait_ge(max_done[0], TILES * i + TILES)
                if j >= 2:
                    pe.wait_ge(exp_done[0], TILES * i + j - 1)
                shifted_scores(0, i, j, (ys, xs)[j % 2])

            def l0_parts(to, g, v):
                for bank, at in halves(to):
                    for c in range(4):
                        j = g * 4 + c
                        last = nc.tensor.matmul(bank[quarter(c), :], v(j), expT[:, j, at],
                                                start=g == 0, stop=g == TILES // 4 - 1)
                return last

            def l0_denominators(i):
                pe.wait_ge(exp_done[0], TILES * i + TILES - 1)
                l0_parts(ys, 0, lambda j: wt("ones0"))
                pe.wait_ge(exp_done[0], TILES * i + TILES)
                l0_parts(ys, 1, lambda j: wt("ones0")).then_inc(d4_mm, 1)

            def l0_values(i):
                l0_parts(xs, 0, lambda j: vT[:, j, C - R:C])
                l0_parts(xs, 1, lambda j: vT[:, j, C - R:C]).then_inc(o_mm[0], 1)

            def l0_end(i, samples_too):
                pe.wait_ge(d4_copied, i + 1)
                for t in range(TILES):
                    last = nc.tensor.matmul(ys[:, t:t + 1], d4[:, t * P:(t + 1) * P], wt("dsum"), start=True, stop=True)
                last.then_inc(d_mm, 1)
                if samples_too:
                    l1_turn(0, 3, xo)
                pe.wait_ge(o4_copied, i + 1)
                project(xs, wt("wp0"), o4, wp_mm)
                pe.wait_ge(inv0_done, i + 1)
                for t in range(TILES):
                    last = nc.tensor.matmul(ys[:, t * P:(t + 1) * P], inv[:, t:t + 1].to_broadcast([P, P]), ident,
                                            start=True, stop=True)
                last.then_inc(inv0_mm, 1)

            def l1_conv1(i, h):
                nc.tensor.matmul((yt, yo)[h][:, :], wt("w1"),
                                 xall[:, bass.ds(i, 1), h * HALF:(h + 1) * HALF].rearrange("p b n -> p (b n)"),
                                 start=True, stop=True).then_inc(conv1_mm, 1)

            def l1_offsets(i, h):
                pe.wait_ge(cells_done, 2 * CORNERS * i + 2 * CORNERS)
                for n, (a, b) in enumerate(PLACES):
                    last = nc.tensor.matmul((yt, yo)[h][quarter(n), :], wt("woff")[:, quarter(n)],
                                            cells[:, h * H // 2 + a:(h + 1) * H // 2 + a, b:b + W],
                                            start=True, stop=True)
                last.then_inc(off4_mm, 1)

            def l1_offsets_turn(i):
                pe.wait_ge(off4_copied, 2 * i + 2)
                for t in range(TILES):
                    last = nc.tensor.matmul(xp[:, t * OFFS:(t + 1) * OFFS], offs4[:, t * P:(t + 1) * P], wt("osum"),
                                            start=True, stop=True)
                last.then_inc(off_mm, 1)

            def l1_table(i):
                flat = cells[:, :, :].rearrange("p a b -> p (a b)")
                for n, (bank, a, b) in enumerate(TABLE_BANKS):
                    if n == 2:
                        pe.wait_ge(off_read, i + 1)
                    for k in range(a, b):
                        rows = P if k < TCHUNKS - 1 else TLAST
                        last = nc.tensor.transpose(bank[0:rows, (k - a) * P:(k - a + 1) * P],
                                                   flat[:, k * P:k * P + rows], ident)
                    last.then_inc(tab_mm, 1)

            def l1_turn(i, t, bank):
                pe.wait_ge(sample_ready, TILES * i + t + 1)
                if t:
                    pe.wait_ge(st_copied, TILES * i + t)
                for g in range(TURNS):
                    last = nc.tensor.transpose(bank[0:TR, g * P:(g + 1) * P], samples[:, t % 2, g * TR:(g + 1) * TR], ident)
                last.then_inc(st_mm, 1)

            def l1_conv2(i, h):
                pe.wait_ge(st_copied, TILES * i + (TILES // 2) * (h + 1))
                bank, at = halves(ys)[h]
                for g in range(TURNS):
                    last = nc.tensor.matmul(bank, wt("w2", TR)[:, g * P:(g + 1) * P], samplesT[:, g, at],
                                            start=g == 0, stop=g == TURNS - 1)
                if h:
                    last.then_inc(w2_mm, 1)

            def l1_conv3(i):
                pe.wait_ge(h2_split, i + 1)
                project(xs, w3_stack[:, :], h2_stack, w3_mm)

            def l2_q(i):
                pe.wait_ge(x_ready[2], i + 1)
                project(xs, wt("wq2"), x2, q_mm[2])

            def l2_k(i):
                project(xq, wt("wk2"), x2, k_mm[2])

            def l2_v(i):
                pe.wait_ge(q_ready[2], i + 1)
                for j in range(TILES):
                    last = nc.tensor.matmul(xs[:, j * C:(j + 1) * C], x2[:, j * P:(j + 1) * P], wt("wv2"),
                                            start=True, stop=True)
                last.then_inc(v_mm[2], 1)

            def l2_scores(i, t):
                if t == 0:
                    pe.wait_ge(k_ready[2], i + 1)
                elif t == 1:
                    pe.wait_ge(v_ready[2], i + 1)
                else:
                    pe.wait_ge(max_done[2], TILES * i + t - 1)
                scores(2, i, t, (xq, xs)[t % 2])

            def l2_shifted(i, j):
                if j == 0:
                    pe.wait_ge(shift_done[2], i + 1)
                if j >= 2:
                    pe.wait_ge(exp_done[2], TILES * i + j - 1)
                shifted_scores(2, i, j, (xs, xq)[j % 2])

            def l2_values(i, t):
                if t == 0:
                    pe.wait_ge(exp_done[2], TILES * i + TILES)
                if t >= 2:
                    pe.wait_ge(o_norm, TILES * i + t - 1)
                weigh_values(2, t, (xo, xp)[t % 2][:, 0:C + 1], C)

            def l2_end(i):
                for t in range(TILES):
                    pe.wait_ge(o_norm, TILES * i + t + 1)
                    last = nc.tensor.transpose(xs[:, t * P:(t + 1) * P], oT[:, t, :], ident)
                last.then_inc(ot_mm, 1)

            def l3_groups(i):
                pe.wait_ge(mom_ready, i + 1)
                nc.tensor.matmul(yo[:, 0:2], wt("gavg"), mom[:, :], start=True, stop=True).then_inc(g_mm, 1)

            def l3_project(i):
                pe.wait_ge(h3_ready, 2 * i + 1)
                project(xs, wt("wq3"), h3, q3_mm)
                project(xq, wt("wk3"), h3, k3_mm)

            def l3_values_in(i, h):
                if h:
                    pe.wait_ge(v3_ready, 2 * i + 1)
                for j in range(TILES // 2):
                    at = (h * TILES // 2 + j) * P
                    last = nc.tensor.matmul(yo[:, j * C:(j + 1) * C], h3[:, at:at + P], u3[:, :], start=True, stop=True)
                last.then_inc(v3_mm, 1)

            def l3_scores(i, t, pair):
                if t == 0:
                    pe.wait_ge(q3_ready, i + 1)
                    pe.wait_ge(k3_ready, i + 1)
                for to, at in halves(pair):
                    last = nc.tensor.matmul(to, q3[:, t * P:(t + 1) * P], k3[:, at], start=True, stop=True)
                last.then_inc(s3_mm, 1)

            def l3_turn(i, t, h, bank):
                if h and bank is yt:
                    pe.wait_ge(pt_act, TILES * i + t + 1)
                elif not h:
                    pe.wait_ge(exp3_done, TILES * i + t + 1)
                for j in range(TILES // 2):
                    at = (h * TILES // 2 + j) * P
                    last = nc.tensor.transpose(bank[:, j * P:(j + 1) * P], probs[:, t % 2, at:at + P], ident)
                last.then_inc(pt_mm, 1)

            def l3_values(i, t):
                pe.wait_ge(pt_act, TILES * i + t + 1)
                pe.wait_ge(pt_dve, TILES * i + t + 1)
                if t:
                    pe.wait_ge(o3_norm, TILES * i + t)
                else:
                    pe.wait_ge(v3_ready, 2 * i + 2)
                for j in range(TILES):
                    last = nc.tensor.matmul(yo[:, 0:C], probsT[:, j * P:(j + 1) * P], v3T[:, j, :],
                                            start=j == 0, stop=j == TILES - 1)
                last.then_inc(o3_mm, 1)

            def l3_end(i):
                pe.wait_ge(o3_norm, TILES * i + TILES)
                for t in range(TILES):
                    last = nc.tensor.transpose(ys[:, t * P:(t + 1) * P], o3T[:, t, :], ident)
                last.then_inc(ot3_mm, 1)

            TABLE_BANKS = ((yt, 0, 4), (yo, 4, 8), (xp, 8, 9))

            def first_loop_step(a, b, following, samples_too=False):
                if b is not None:
                    pe.wait_ge(x1_ready, b + 1)
                for t in range(TILES):
                    l0_scores(a, t)
                    if t in (3, 4):
                        l0_values_in(a, t - 3)
                    if b is not None and t in (1, 2):
                        l1_conv1(b, t - 1)
                    if b is not None and t == 6:
                        l1_offsets(b, 0)
                if b is not None:
                    l1_offsets(b, 1)
                l0_shift(a)
                for j in range(TILES):
                    l0_shifted(a, j)
                    if b is not None and j == 1:
                        l1_offsets_turn(b)
                    if b is not None and j == 4:
                        l1_table(b)
                pe.wait_ge(v_ready[0], a + 1)
                if samples_too:
                    l1_turn(0, 0, xo)
                l0_denominators(a)
                if samples_too:
                    l1_turn(0, 1, xo)
                l0_values(a)
                if samples_too:
                    l1_turn(0, 2, xo)
                l0_end(a, samples_too)
                if b is not None:
                    pe.wait_ge(tab_copied, 3 * b + 3)
                if following is not None:
                    l0_project(following)

            def second_loop_step(a, b, c):
                L3, L2, SAMPLES = a is not None, b is not None, c is not None
                score_banks = (ys, ys) if L2 else (ys, xs)
                turn_banks = (yt, yt) if L2 else (yt, xp)
                if L2:
                    l1_conv2(b, 1)
                if L3:
                    l3_groups(a)
                if L2 and not L3:
                    l1_table(BATCH - 1)
                    pe.wait_ge(tab_copied, 3 * BATCH)
                if L3:
                    l3_project(a)
                    l3_values_in(a, 0)
                    if L2:
                        pe.wait_ge(h2_high, 2 * b + 2)
                    l3_scores(a, 0, ys)
                    l3_values_in(a, 1)
                for t in range(TILES):
                    if L3:
                        if t + 1 < TILES:
                            if L2:
                                pe.wait_ge(exp3_done, TILES * a + t + 1)
                            elif t:
                                pe.wait_ge(exp3_done, TILES * a + t)
                            l3_scores(a, t + 1, score_banks[(t + 1) % 2])
                        l3_turn(a, t, 0, turn_banks[0])
                    if L2:
                        if t == 0:
                            l1_conv3(b)
                        if t == 1:
                            l2_q(b)
                        if t == 2:
                            l2_v(b)
                        if t == 3:
                            l2_scores(b, 1)
                        if t == 4:
                            l2_scores(b, 4)
                        if t == 5:
                            l2_scores(b, 7)
                        if t == 6:
                            l2_shifted(b, 0)
                        if t == 7:
                            l2_shifted(b, 3)
                    if L3:
                        l3_turn(a, t, 1, turn_banks[1])
                    if L2:
                        if t == 1:
                            l2_k(b)
                        if t == 2:
                            l2_scores(b, 0)
                        if t == 3:
                            l2_scores(b, 2)
                        if t == 4:
                            l2_scores(b, 5)
                        if t == 6:
                            l2_shifted(b, 1)
                        if t == 7:
                            l2_shifted(b, 4)
                    if L3:
                        l3_values(a, t)
                    if L2:
                        if t == 3:
                            l2_scores(b, 3)
                        if t == 4:
                            l2_scores(b, 6)
                        if t == 5:
                            shift_rows(2, b, xq)
                        if t == 6:
                            l2_shifted(b, 2)
                        if t == 7:
                            l2_shifted(b, 5)
                if L3:
                    l3_end(a)
                if L2:
                    l2_shifted(b, 6)
                    if SAMPLES:
                        l1_turn(c, 0, yt)
                    l2_shifted(b, 7)
                    if SAMPLES:
                        l1_turn(c, 1, yt)
                    if SAMPLES:
                        l1_turn(c, 2, yt)
                    for n in range(TILES):
                        l2_values(b, n)
                        if SAMPLES and n in (1, 3, 5, 7):
                            l1_turn(c, 3 + n // 2, yt)
                        if SAMPLES and n == 6:
                            if L3:
                                pe.wait_ge(y_ready, a + 2)
                            l1_conv2(c, 0)
                    l2_end(b)
                    if SAMPLES:
                        l1_turn(c, TILES - 1, yt)
                    pe.wait_ge(x3_ready, b + 1)

            pe.wait_ge(weights0_in, 16)
            l0_project(0)
            first_loop_step(0, None, 1)
            pe.wait_ge(weights_in, 16)
            with pe.Fori(0, BATCH - 2) as i:
                first_loop_step(i + 1, i, i + 2)
            first_loop_step(BATCH - 1, BATCH - 2, None, samples_too=True)
            pe.wait_ge(x1_ready, BATCH)
            nc.tensor.matmul(ys[:, 0:C], wt("wvT3"), wt("wp3"), start=True, stop=True)
            nc.tensor.matmul(ys[:, C:2 * C], wt("bv3"), wt("wp3"), start=True, stop=True).then_inc(setup_pe, 1)
            for h in range(2):
                l1_conv1(BATCH - 1, h)
            l1_turn(0, 4, xo)
            l1_turn(0, 5, xo)
            for h in range(2):
                l1_offsets(BATCH - 1, h)
            l1_turn(0, 6, xo)
            pe.wait_ge(setup_act, 2)
            l1_conv2(0, 0)
            l1_turn(0, 7, xo)
            l1_offsets_turn(BATCH - 1)
            second_loop_step(None, 0, 1)
            with pe.Fori(0, BATCH - 2) as i:
                second_loop_step(i, i + 1, i + 2)
            second_loop_step(BATCH - 2, BATCH - 1, None)
            second_loop_step(BATCH - 1, None, None)

        @block.scalar
        def _(act):
            def copy(to, bank):
                return nc.scalar.activation(to, bank, ACT.Copy)

            def exponentials(L, i, j, bank):
                act.wait_ge(t_mm[L], TILES * i + j + 1)
                nc.scalar.activation(expT[:, j, :], bank[:, :], ACT.Exp).then_inc(exp_done[L], 1)

            def shift_copy(L, i, bank):
                act.wait_ge(shift_mm[L], i + 1)
                copy(q_stack[quarter(3), :], bank[quarter(3), :]).then_inc(shift_done[L], 1)

            def l0_project(i):
                act.wait_ge(q_mm[0], i + 1)
                nc.scalar.activation(q_stack[0:3 * R, :], xq[0:3 * R, :], ACT.Copy, scale=float(R) ** -0.5)\
                    .then_inc(q_high[0], 1)
                act.wait_ge(k_mm[0], i + 1)
                copy(k_stack[0:3 * R, :], yy[0:3 * R, :]).then_inc(k_high[0], 1)

            def l0_values_in(i):
                act.wait_ge(v_mm[0], i + 1)
                copy(vT[:, :, C - R:C], xo[:, 0:TILES * R].rearrange("p (j r) -> p j r", r=R)).then_inc(v_ready[0], 1)

            def l0_end(i):
                act.wait_ge(o_mm[0], i + 1)
                copy(o4, xs[:, :]).then_inc(o4_copied, 1)

            def l0_next(i):
                copy(xcur[:, :], xall[:, bass.ds(i, 1), :].rearrange("p b n -> p (b n)")).then_inc(x_ready[0], 1)

            def l1_cells(i):
                for h, bank in enumerate((yt, yo)):
                    act.wait_ge(conv1_mm, 2 * i + h + 1)
                    for c in range(CORNERS):
                        dy, dx = c // 2, c % 2
                        at = slice(1 - dy + h * H // 2, 1 - dy + (h + 1) * H // 2)
                        nc.scalar.activation(cells[quarter(c), at, 1 - dx:1 - dx + W],
                                             bank[quarter(c), :].rearrange("p (a b) -> p a b", b=W), ACT.Relu,
                                             bias=bn_t[quarter(c), 0:1], scale=bn_s[quarter(c), 0:1]).then_inc(cells_done, 1)

            def l1_offsets(i, h):
                act.wait_ge(off4_mm, 2 * i + h + 1)
                nc.scalar.activation(offs4[:, h * HALF:(h + 1) * HALF], (yt, yo)[h][:, :], ACT.Identity,
                                     bias=wt("boff")).then_inc(off4_copied, 1)

            def l1_mask(i):
                act.wait_ge(off_read, i + 1)
                nc.scalar.activation(mexp[:, :, :], offs[:, :, YX:OFFS], ACT.Exp, scale=-1.0).then_inc(mask_exp, 1)

            def l1_table(i):
                for n, (bank, a, b) in enumerate(((yt, 0, 4), (yo, 4, 8), (xp, 8, 9))):
                    rows = P if n < 2 else TLAST
                    act.wait_ge(tab_mm, 3 * i + n + 1)
                    to = tabS[0:rows, bass.ds(i, 1), a:b, :].rearrange("p i k d -> p (i k) d")
                    copy(to, bank[0:rows, 0:(b - a) * P].rearrange("p (k d) -> p k d", d=P)).then_inc(tab_copied, 1)

            def l1_turn(i, t, bank):
                act.wait_ge(st_mm, TILES * i + t + 1)
                copy(samplesT[:, :, t * P:(t + 1) * P],
                     bank[0:TR, 0:TURNS * P].rearrange("p (g n) -> p g n", g=TURNS)).then_inc(st_copied, 1)

            def l1_conv2(i, parts=(0, 1)):
                act.wait_ge(w2_mm, i + 1)
                for n in parts:
                    to = (h2_full, h2_stack)[n]
                    nc.scalar.activation(to[:, :], ys[:, :], ACT.Relu, bias=bn_t[:, 1:2], scale=bn_s[:, 1:2])\
                        .then_inc(h2_high, 1)

            def l1_end(i):
                act.wait_ge(x2_added, i + 1)
                nc.scalar.activation(x2[:, :], x2_sum[:, :], ACT.Relu, bias=bn_t[:, 2:3]).then_inc(x_ready[2], 1)

            def l2_q(i):
                act.wait_ge(q_mm[2], i + 1)
                nc.scalar.activation(q_stack[0:3 * R, :], xs[0:3 * R, :], ACT.Identity, bias=wt("bq2")[0:3 * R, :])\
                    .then_inc(q_high[2], 1)

            def l2_k(i):
                act.wait_ge(k_mm[2], i + 1)
                nc.scalar.activation(k_stack[0:3 * R, :], xq[0:3 * R, :], ACT.Identity, bias=wt("bk2")[0:3 * R, :])\
                    .then_inc(k_high[2], 1)

            def l3_norm(i):
                act.wait_ge(gvar_ready, i + 1)
                nc.scalar.activation(gstd[:, :], gvar[:, :], ACT.Sqrt).then_inc(gstd_ready, 1)
                act.wait_ge(gaff_ready, i + 1)
                nc.scalar.activation(h3[:, :], x3[:, :], ACT.Identity, bias=gbias[:, :], scale=gscale[:, :])\
                    .then_inc(h3_ready, 1)

            def l3_residual(i):
                act.wait_ge(y_out, 16 * i + 16)
                nc.scalar.activation(x3s[:, :], x3[:, :], ACT.Identity, bias=bp3s[:, :], scale=2.0 ** -0.5)\
                    .then_inc(h3_ready, 1)

            def l3_q(i):
                act.wait_ge(q3_mm, i + 1)
                nc.scalar.activation(q3[:, :], xs[:, :], ACT.Identity, bias=bq3s[:, :], scale=float(C) ** -0.5)\
                    .then_inc(q3_ready, 1)

            def l3_k(i):
                act.wait_ge(k3_mm, i + 1)
                nc.scalar.activation(k3[:, :], xq[:, :], ACT.Identity, bias=wt("bk3")).then_inc(k3_ready, 1)

            def l3_exp(i, t, pair):
                act.wait_ge(max3_done, TILES * i + t + 1)
                if t >= 2:
                    act.wait_ge(pt_mm, 2 * TILES * i + 2 * (t - 1))
                nc.scalar.activation(probs[:, t % 2, :], pair[:, :], ACT.Exp, bias=neg_max3[:, t:t + 1],
                                     accum_out=denom3[:, t:t + 1]).then_inc(exp3_done, 1)

            def l3_turn(i, t):
                act.wait_ge(pt_mm, 2 * TILES * i + 2 * t + 1)
                copy(probsT[:, 0:HALF], yt[:, :]).then_inc(pt_act, 1)

            def first_loop_step(a, b, following, samples_too=False):
                if b is not None:
                    l1_cells(b)
                l0_values_in(a)
                if b is not None:
                    l1_offsets(b, 0)
                shift_copy(0, a, xs)
                if b is not None:
                    l1_offsets(b, 1)
                for j in range(TILES):
                    exponentials(0, a, j, (ys, xs)[j % 2])
                    if b is not None and j == 3:
                        l1_mask(b)
                    if b is not None and j == 5:
                        l1_table(b)
                if samples_too:
                    l1_turn(0, 0, xo)
                    l1_turn(0, 1, xo)
                if following is not None:
                    l0_next(following)
                l0_end(a)
                if samples_too:
                    l1_turn(0, 2, xo)
                    l1_turn(0, 3, xo)
                if following is not None:
                    l0_project(following)

            def second_loop_step(a, b, c):
                L3, L2, SAMPLES = a is not None, b is not None, c is not None
                if L3:
                    l3_norm(a)
                if L2:
                    l1_conv2(b, (0,))
                if L3:
                    l3_q(a)
                if L2:
                    l1_conv2(b, (1,))
                if L2 and not L3:
                    l1_mask(BATCH - 1)
                    l1_table(BATCH - 1)
                if L3:
                    l3_k(a)
                    l3_residual(a)
                    l3_exp(a, 0, ys)
                for t in range(TILES):
                    if L3:
                        l3_turn(a, t)
                        if t + 1 < TILES:
                            l3_exp(a, t + 1, (ys if L2 else (ys, xs)[(t + 1) % 2]))
                    if L2:
                        if t == 0:
                            l1_end(b)
                        if t == 1:
                            l2_q(b)
                            l2_k(b)
                        if t == 5:
                            shift_copy(2, b, xq)
                        if t in (6, 7):
                            for n in range(3 * t - 18, 3 * t - 15):
                                exponentials(2, b, n, (xs, xq)[n % 2])
                if L2:
                    exponentials(2, b, 6, xs)
                    if SAMPLES:
                        l1_turn(c, 0, yt)
                    exponentials(2, b, 7, xq)
                    if SAMPLES:
                        for t in range(1, TILES):
                            l1_turn(c, t, yt)

            act.dma_start(xall[:, 0, :], x_view[0]).then_inc(x_in[0], 16)
            act.dma_start(wts[:, FIRST:WIDTH], weights_dram[:, FIRST:WIDTH]).then_inc(weights_in, 16)
            act.wait_ge(weights0_in, 16)
            l0_project(0)
            act.wait_ge(x_in[1], 16)
            first_loop_step(0, None, 1)
            act.wait_ge(setup_dve, 1)
            nc.scalar.activation(bn_std[:, :], bn_std[:, :], ACT.Sqrt).then_inc(setup_sqrt, 1)
            act.wait_ge(setup_dve, 2)
            for b in range(2, BATCH):
                act.wait_ge(x_in[b], 16)
            with act.Fori(0, BATCH - 2) as i:
                first_loop_step(i + 1, i, i + 2)
            first_loop_step(BATCH - 1, BATCH - 2, None, samples_too=True)
            act.wait_ge(setup_pe, 1)
            for n, to in enumerate((u3, bvp3)):
                copy(to[:, :], ys[:, n * C:(n + 1) * C]).then_inc(setup_act, 1)
            l1_cells(BATCH - 1)
            l1_turn(0, 4, xo)
            l1_turn(0, 5, xo)
            for h in range(2):
                l1_offsets(BATCH - 1, h)
            l1_turn(0, 6, xo)
            l1_turn(0, 7, xo)
            second_loop_step(None, 0, 1)
            with act.Fori(0, BATCH - 2) as i:
                second_loop_step(i, i + 1, i + 2)
            second_loop_step(BATCH - 2, BATCH - 1, None)
            second_loop_step(BATCH - 1, None, None)

        @block.vector
        def _(dve):
            def low_part(stack, c, bank, n, before, high, done, op=ALU.add):
                dve.wait_ge(high, n)
                nc.vector.scalar_tensor_tensor(stack[quarter(c), :], bank[quarter(c), :], before,
                                               stack[quarter(c), :].bitcast(fp32), op, ALU.subtract).then_inc(done, 1)

            def maximum(L, i, t, bank):
                dve.wait_ge(s_mm[L], TILES * i + t + 1)
                nc.vector.tensor_reduce(neg_max[:, t:t + 1], bank[:, :], axis=X, op=ALU.max,
                                        negate=True).then_inc(max_done[L], 1)

            def shift_parts(L, i):
                dve.drain()
                nc.vector.tensor_copy(shift[:, :, 0:1], neg_max[:, :].rearrange("p (t a) -> p t a", a=1))
                dve.drain()
                nc.vector.tensor_tensor(shift[:, :, 1:2], neg_max[:, :].rearrange("p (t a) -> p t a", a=1),
                                        shift[:, :, 0:1], ALU.subtract).then_inc(shift_ready[L], 1)

            def l0_project(i):
                low_part(q_stack, 2, xq, i + 1, float(R) ** -0.5, q_high[0], q_ready[0], ALU.mult)
                low_part(k_stack, 1, yy, i + 1, 0.0, k_high[0], k_ready[0])

            def l0_denominators(i, samples_too):
                dve.wait_ge(d4_mm, i + 1)
                nc.vector.tensor_copy(d4, ys[:, :]).then_inc(d4_copied, 1)
                if samples_too:
                    l1_samples(0, 3)
                dve.wait_ge(d_mm, i + 1)
                nc.vector.reciprocal(inv[:, :], ys[:, 0:TILES]).then_inc(inv0_done, 1)
                if samples_too:
                    l1_samples(0, 4)

            def l0_end(i):
                dve.wait_ge(inv0_mm, i + 1)
                nc.vector.tensor_copy(inv0, ys[:, :])
                dve.drain()
                dve.wait_ge(wp_mm, i + 1)
                nc.vector.tensor_tensor(inv0, xs[:, :], inv0, ALU.mult)
                dve.drain()
                x = xall[:, bass.ds(i, 1), :].rearrange("p b n -> p (b n)")
                nc.vector.tensor_tensor(x, inv0, x, ALU.add).then_inc(x1_ready, 1)

            def l1_coordinates(i):
                dve.wait_ge(off_mm, i + 1)
                nc.vector.tensor_copy(offs[:, :, :], xp[:, 0:TILES * OFFS].rearrange("p (t k) -> p t k", k=OFFS))\
                    .then_inc(off_read, 1)
                dve.drain()
                nc.vector.tensor_tensor(yx[:, :, :], offs[:, :, 0:YX],
                                        wt("base").rearrange("p (t k) -> p t k", k=YX), ALU.add)
                dve.drain()
                nc.vector.tensor_scalar(yx[:, :, :], yx[:, :, :], -1.0, float(H), ALU.max, ALU.min)
                dve.drain()
                nc.vector.tensor_scalar(low[:, :, :], yx[:, :, :], 0.5, ROUND, ALU.add, ALU.add)
                dve.drain()
                nc.vector.tensor_scalar(low[:, :, :], low[:, :, :], ROUND, None, ALU.subtract)
                dve.drain()
                nc.vector.scalar_tensor_tensor(rows_all[:, bass.ds(i, 1), :].rearrange("p b (t k) -> p (b t) k", k=TAPS),
                                               low[:, :, 0:TAPS], float(CELLS), low[:, :, TAPS:YX],
                                               ALU.mult, ALU.add).then_inc(rows_ready, 1)
                nc.vector.scalar_tensor_tensor(frac[:, :, :], yx[:, :, :], 1.0, low[:, :, :], ALU.add, ALU.subtract)
                dve.drain()
                nc.vector.tensor_scalar(rest[:, :, :], frac[:, :, :], -1.0, 1.0, ALU.mult, ALU.add)
                dve.wait_ge(mask_exp, i + 1)
                nc.vector.tensor_scalar(mask[:, :, :], mexp[:, :, :], 1.0, None, ALU.add)
                dve.drain()
                nc.vector.reciprocal(mask[:, :, :], mask[:, :, :])
                dve.drain()
                for dy, part in enumerate((rest, frac)):
                    nc.vector.tensor_tensor(wy[:, dy, :, :], part[:, :, 0:TAPS], mask[:, :, :], ALU.mult)
                dve.drain()
                for c in range(CORNERS):
                    part = (rest, frac)[c % 2]
                    to = corner_w[:, bass.ds(i, 1), :, :].rearrange("p b t (k c) -> p (b t k) c", c=CORNERS)[:, :, c]
                    last = nc.vector.tensor_tensor(to.rearrange("p (t k) -> p t k", k=TAPS), wy[:, c // 2, :, :],
                                                   part[:, :, TAPS:YX], ALU.mult)
                last.then_inc(corner_ready, 1)

            def l1_samples(i, t):
                dve.wait_ge(got_sem[t], 16 * TAPS * (i + 1))
                w = corner_w[:, bass.ds(i, 1), t, :].rearrange("p b k -> p (b k)")
                nc.vector.tensor_tensor(weighed[:, :, :].rearrange("p k (c r) -> p (k c) r", r=R),
                                        got[:, t, :, :].rearrange("p k (c r) -> p (k c) r", r=R),
                                        w.rearrange("p (k a) -> p k a", a=1).to_broadcast([P, TAPS * CORNERS, R]),
                                        ALU.mult).then_inc(slot_free, 1)
                dve.drain()
                if t == TILES - 1:
                    dve.sem_inc(table_free, 1)
                if t >= 2:
                    dve.wait_ge(st_mm, TILES * i + t - 1)
                nc.vector.tensor_reduce(samples[:, t % 2, :].rearrange("p (k r) -> p k r", r=R),
                                        weighed[:, :, :].rearrange("p k (c r) -> p k r c", r=R),
                                        axis=X, op=ALU.add).then_inc(sample_ready, 1)
                dve.drain()

            def l1_conv2(i):
                dve.wait_ge(h2_high, 2 * i + 2)
                nc.vector.tensor_tensor(h2_stack[quarter(2, 2), :], h2_full[quarter(2, 2), :],
                                        h2_stack[quarter(2, 2), :].bitcast(fp32), ALU.subtract).then_inc(h2_split, 1)

            def l1_end(i):
                dve.wait_ge(w3_mm, i + 1)
                nc.vector.scalar_tensor_tensor(x2_sum[:, :], xs[:, :], bn_s[:, 2:3],
                                               xall[:, bass.ds(i, 1), :].rearrange("p b n -> p (b n)"),
                                               ALU.mult, ALU.add).then_inc(x2_added, 1)

            def l2_v(i):
                dve.wait_ge(v_mm[2], i + 1)
                nc.vector.tensor_tensor(vT[:, :, 0:C], xs[:, :].rearrange("p (j c) -> p j c", c=C),
                                        wt("bv2").rearrange("p (a c) -> p a c", a=1).to_broadcast([P, TILES, C]),
                                        ALU.add).then_inc(v_ready[2], 1)

            def l2_values(i, t):
                dve.wait_ge(o_mm[2], TILES * i + t + 1)
                bank = (xo, xp)[t % 2]
                nc.vector.reciprocal(inv[:, t:t + 1], bank[:, C:C + 1])
                dve.drain()
                nc.vector.tensor_scalar(oT[:, t, :], bank[:, 0:C], inv[:, t:t + 1], None, ALU.mult).then_inc(o_norm, 1)

            def l2_end(i):
                dve.wait_ge(ot_mm, i + 1)
                nc.vector.scalar_tensor_tensor(x3[:, :], xs[:, :], wt("gamma"), x2[:, :], ALU.mult,
                                               ALU.add).then_inc(x3_ready, 1)

            def l3_moments(i):
                dve.drain()
                for h in range(2):
                    nc.vector.bn_stats(stats[:, h, :], x3[:, h * HALF:(h + 1) * HALF])
                dve.drain()
                nc.vector.bn_aggr(mom[:, :], stats[:, :, :].rearrange("p h s -> p (h s)"))
                dve.drain()
                nc.vector.scalar_tensor_tensor(mom[:, 1:2], mom[:, 0:1], mom[:, 0:1], mom[:, 1:2], ALU.mult,
                                               ALU.add).then_inc(mom_ready, 1)

            def l3_norm(i):
                dve.wait_ge(g_mm, i + 1)
                nc.vector.tensor_copy(gmom[:, :], yo[:, 0:2])
                dve.drain()
                nc.vector.tensor_scalar(gsq[:, :], gmom[:, 0:1], gmom[:, 0:1], EPS, ALU.mult, ALU.subtract)
                dve.drain()
                nc.vector.tensor_tensor(gvar[:, :], gmom[:, 1:2], gsq[:, :], ALU.subtract).then_inc(gvar_ready, 1)
                dve.wait_ge(gstd_ready, i + 1)
                nc.vector.reciprocal(gscale[:, :], gstd[:, :])
                dve.drain()
                nc.vector.tensor_tensor(gscale[:, :], gscale[:, :], wt("gn_w"), ALU.mult)
                dve.drain()
                nc.vector.tensor_tensor(gbias[:, :], gmom[:, 0:1], gscale[:, :], ALU.mult)
                dve.drain()
                nc.vector.tensor_tensor(gbias[:, :], wt("gn_b"), gbias[:, :], ALU.subtract).then_inc(gaff_ready, 1)

            def l3_values_in(i, h):
                dve.wait_ge(v3_mm, 2 * i + h + 1)
                nc.vector.tensor_tensor(v3T[:, h * TILES // 2:(h + 1) * TILES // 2, :],
                                        yo[:, :].rearrange("p (j c) -> p j c", c=C),
                                        bvp3[:, :].rearrange("p (a c) -> p a c", a=1).to_broadcast([P, TILES // 2, C]),
                                        ALU.add).then_inc(v3_ready, 1)

            def l3_max(i, t, pair):
                dve.wait_ge(s3_mm, TILES * i + t + 1)
                nc.vector.tensor_reduce(neg_max3[:, t:t + 1], pair[:, :], axis=X, op=ALU.max,
                                        negate=True).then_inc(max3_done, 1)

            def l3_turn(i, t, bank):
                dve.wait_ge(exp3_done, TILES * i + t + 1)
                nc.vector.reciprocal(inv3[:, t:t + 1], denom3[:, t:t + 1]).then_inc(inv3_done, 1)
                dve.wait_ge(pt_mm, 2 * TILES * i + 2 * t + 2)
                nc.vector.tensor_copy(probsT[:, HALF:N], bank[:, :]).then_inc(pt_dve, 1)

            def l3_values(i, t):
                dve.wait_ge(o3_mm, TILES * i + t + 1)
                dve.wait_ge(inv3_done, TILES * i + t + 1)
                nc.vector.tensor_scalar(o3T[:, t, :], yo[:, 0:C], inv3[:, t:t + 1], None, ALU.mult).then_inc(o3_norm, 1)

            def l3_end(i):
                dve.wait_ge(ot3_mm, i + 1)
                dve.wait_ge(h3_ready, 2 * i + 2)
                nc.vector.scalar_tensor_tensor(y[:, :], ys[:, :], 2.0 ** -0.5, x3s[:, :], ALU.mult,
                                               ALU.add).then_inc(y_ready, 1)

            def first_loop_step(a, b, following, samples_too=False):
                for t in range(TILES):
                    maximum(0, a, t, (xs, ys)[t % 2])
                shift_parts(0, a)
                if b is not None:
                    l1_coordinates(b)
                if samples_too:
                    for t in range(3):
                        l1_samples(0, t)
                l0_denominators(a, samples_too)
                l0_end(a)
                if following is not None:
                    l0_project(following)

            def second_loop_step(a, b, c):
                L3, L2, SAMPLES = a is not None, b is not None, c is not None
                if L3:
                    l3_moments(a)
                    l3_norm(a)
                    l3_values_in(a, 0)
                if L2 and not L3:
                    l1_coordinates(BATCH - 1)
                if L2:
                    l1_conv2(b)
                if L3:
                    l3_max(a, 0, ys)
                    l3_values_in(a, 1)
                for t in range(TILES):
                    if L2:
                        if t == 4:
                            maximum(2, b, 3, xs)
                        if t == 5:
                            maximum(2, b, 6, xq)
                    if L3:
                        if t + 1 < TILES:
                            l3_max(a, t + 1, (ys if L2 else (ys, xs)[(t + 1) % 2]))
                        l3_turn(a, t, yt if L2 else xp)
                    if L2:
                        if t == 0:
                            l1_end(b)
                        if t == 2:
                            l2_v(b)
                        if t == 3:
                            maximum(2, b, 1, xs)
                        if t == 4:
                            maximum(2, b, 4, xq)
                        if t == 5:
                            maximum(2, b, 7, xs)
                            shift_parts(2, b)
                    if L3:
                        l3_values(a, t)
                    if L2:
                        if t == 1:
                            low_part(q_stack, 2, xs, b + 1, wt("bq2")[quarter(2), :], q_high[2], q_ready[2])
                            low_part(k_stack, 1, xq, b + 1, wt("bk2")[quarter(1), :], k_high[2], k_ready[2])
                        if t == 2:
                            maximum(2, b, 0, xq)
                        if t == 3:
                            maximum(2, b, 2, xq)
                        if t == 4:
                            maximum(2, b, 5, xs)
                    if SAMPLES and t in (6, 7):
                        l1_samples(c, t - 6)
                if L3:
                    l3_end(a)
                if SAMPLES:
                    l1_samples(c, 2)
                    l1_samples(c, 3)
                if L2:
                    for n in range(TILES):
                        l2_values(b, n)
                        if SAMPLES and n in (0, 2, 4, 5):
                            l1_samples(c, {0: 4, 2: 5, 4: 6, 5: 7}[n])
                    l2_end(b)

            nc.vector.memset(cells[:, :, :], 0.0)
            nc.vector.memset(shift[:, :, :], 0.0)
            nc.vector.memset(vT[:, :, C:C + 1], 1.0)
            dve.sem_inc(slot_free, TILES)
            dve.sem_inc(table_free, 2)
            dve.sem_inc(y_ready, 1)
            dve.sem_inc(y_out, 16)
            dve.wait_ge(weights0_in, 16)
            nc.vector.tensor_copy(ident16[:, :], ident)
            nc.vector.tensor_copy(k_stack[quarter(3), :], wt("ones")[quarter(3), :].to_broadcast([R, N]))
            dve.wait_ge(x_in[0], 16)
            nc.vector.tensor_copy(xcur[:, :], xall[:, 0, :]).then_inc(x_ready[0], 1)
            l0_project(0)
            first_loop_step(0, None, 1)
            dve.wait_ge(weights_in, 16)
            nc.vector.tensor_scalar(bn_std[:, :], wt("bn_v"), EPS, None, ALU.add).then_inc(setup_dve, 1)
            nc.vector.tensor_copy(w3_stack[:, :], wt("w3"))
            nc.vector.tensor_scalar(bq3s[:, :], wt("bq3"), float(C) ** -0.5, None, ALU.mult)
            nc.vector.tensor_scalar(bp3s[:, :], wt("bp3"), 2.0 ** -0.5, None, ALU.mult)
            dve.drain()
            for c in (1, 3):
                nc.vector.tensor_tensor(w3_stack[quarter(c), :], wt("w3")[quarter(c), :],
                                        w3_stack[quarter(c), :].bitcast(fp32), ALU.subtract)
            dve.wait_ge(setup_sqrt, 1)
            nc.vector.reciprocal(bn_s[:, :], bn_std[:, :])
            dve.drain()
            nc.vector.tensor_tensor(bn_s[:, :], bn_s[:, :], wt("bn_g"), ALU.mult)
            dve.drain()
            nc.vector.tensor_tensor(bn_t[:, :], wt("bn_m"), bn_s[:, :], ALU.mult)
            dve.drain()
            nc.vector.tensor_tensor(bn_t[:, :], wt("bn_b"), bn_t[:, :], ALU.subtract)
            dve.drain()
            nc.vector.scalar_tensor_tensor(bn_t[:, 1:2], bn_s[:, 1:2], wt("dcn_b"), bn_t[:, 1:2], ALU.mult,
                                           ALU.add).then_inc(setup_dve, 1)
            for b in range(1, BATCH):
                dve.wait_ge(x_in[b], 16)
            with dve.Fori(0, BATCH - 2) as i:
                first_loop_step(i + 1, i, i + 2)
            dve.wait_ge(corner_ready, 1)
            first_loop_step(BATCH - 1, BATCH - 2, None, samples_too=True)
            for t in range(5, TILES):
                l1_samples(0, t)
            dve.wait_ge(corner_ready, BATCH - 1)
            second_loop_step(None, 0, 1)
            with dve.Fori(0, BATCH - 2) as i:
                second_loop_step(i, i + 1, i + 2)
            second_loop_step(BATCH - 2, BATCH - 1, None)
            second_loop_step(BATCH - 1, None, None)


def pack(a):
    w = np.zeros((P, WIDTH), np.float32)

    def put(name, value):
        value = np.asarray(value, np.float32)
        value = value.reshape(value.shape[0], -1)
        w[:value.shape[0], AT[name][0]:AT[name][1]] = value

    def column(v):
        return np.asarray(v).reshape(-1, 1)

    four = lambda v: np.concatenate([v] * 4, axis=0)
    put("ident", np.eye(P))
    put("wq0", four(a["L0_conv_Wq"]).T)
    put("wk0", four(a["L0_conv_Wk"]).T)
    put("wv0", a["L0_conv_Wv"].T)
    put("wp0", four(a["L0_conv_Wp"].T))
    put("ones", (np.arange(P) // 2 == 3 * R // 2)[:, None])
    put("ones0", np.ones((P, R)))
    put("dsum", (np.arange(P) % R == 0)[:, None])
    put("w1", four(a["L1_conv_w1"]).T)
    for n, (name, k) in enumerate((("bn_g", "g"), ("bn_b", "b"), ("bn_m", "m"), ("bn_v", "v"))):
        put(name, np.concatenate([column(four(a[f"L1_conv_bn1_{k}"])), column(four(a[f"L1_conv_bn2_{k}"])),
                                  column(a[f"L1_conv_bn3_{k}"])], axis=1))
    put("dcn_b", column(four(a["L1_conv_dcn_b"])))
    order = [2 * k for k in range(TAPS)] + [2 * k + 1 for k in range(TAPS)] + list(range(YX, OFFS))
    woff = a["L1_conv_woff"][order]
    to = np.zeros((CORNERS, R, 4, R), np.float32)
    for n, (oy, ox) in enumerate(PLACES):
        for c in range(CORNERS):
            ky, kx = oy + c // 2, ox + c % 2
            if (oy == 0 or ky == 2) and (ox == 0 or kx == 2):
                to[c, :, n, :OFFS] = woff[:, :, ky, kx].T
    put("woff", to.reshape(P, -1))
    put("boff", column(a["L1_conv_boff"][order]))
    put("osum", np.concatenate([np.eye(R, OFFS)] * 4, axis=0))
    p, t, k = np.arange(P)[:, None, None], np.arange(TILES)[None, :, None], np.arange(TAPS)[None, None, :]
    by, bx = t * ROWS + p // W - 1 + k // 3, p % W - 1 + k % 3 + 0 * t
    put("base", np.concatenate([by, bx], axis=2))
    w2 = a["L1_conv_w2"].reshape(R, R, TURNS, TAPS_A_TURN).transpose(3, 1, 2, 0)
    put("w2", np.concatenate([w2] * 4, axis=3).reshape(TR, TURNS * P))
    put("w3", four(a["L1_conv_w3"].T))
    pad = lambda v: four(np.concatenate([v, np.zeros((R - QK2,) + v.shape[1:], np.float32)], axis=0))
    put("wq2", pad(a["L2_conv_wq"]).T)
    put("wk2", pad(a["L2_conv_wk"]).T)
    put("wv2", a["L2_conv_wv"].T)
    put("bq2", column(pad(a["L2_conv_bq"])))
    put("bk2", column(pad(a["L2_conv_bk"])))
    put("bv2", np.broadcast_to(a["L2_conv_bv"], (P, C)))
    put("gamma", column(a["L2_conv_gamma"]))
    put("wq3", a["L3_conv_Wq"])
    put("wk3", a["L3_conv_Wk"])
    put("wvT3", a["L3_conv_Wv"].T)
    put("wp3", a["L3_conv_Wp"])
    for k in ("bq", "bk", "bp"):
        put(k + "3", column(a["L3_conv_" + k]))
    put("bv3", np.broadcast_to(column(a["L3_conv_bv"]), (C, P)))
    put("gn_w", column(a["L3_conv_gn_w"]))
    put("gn_b", column(a["L3_conv_gn_b"]))
    put("gavg", np.kron(np.eye(C // GROUP), np.full((GROUP, GROUP), 1.0 / GROUP)))
    return w


def kernel(**inputs):
    import concourse.bacc as bacc
    from concourse.bass_utils import run_bass_kernel_spmd

    a = {k: np.asarray(v) for k, v in inputs.items()}
    x, w = np.ascontiguousarray(a["x"]), pack(a)
    nc = bacc.Bacc("TRN2", target_bir_lowering=False, num_devices=1)
    fp32 = mybir.dt.float32
    x_ap = nc.dram_tensor("x_dram", x.shape, fp32, kind="ExternalInput").ap()
    w_ap = nc.dram_tensor("weights_dram", w.shape, fp32, kind="ExternalInput").ap()
    o_ap = nc.dram_tensor("out_dram", x.shape, fp32, kind="ExternalOutput").ap()
    build(nc, x_ap, w_ap, o_ap)
    result = run_bass_kernel_spmd(nc, [{"x_dram": x, "weights_dram": w}], core_ids=[0])
    return result.results[0]["out_dram"]
```

```python
import numpy as np
import concourse.bass as bass
from concourse import mybir
from contextlib import ExitStack

BATCH, C, H, W = 4, 128, 32, 32
N = H * W
P = 128
TILES = N // P
ROWS = P // W
HALF = 512
R = 32
QK2 = C // 8
TAPS = 9
CORNERS = 4
GROUP = C // 32
EPS = 1e-5
CELLS = H + 1
TABLE = CELLS * CELLS
TCHUNKS = -(-TABLE // P)
TLAST = TABLE - (TCHUNKS - 1) * P
YX = 2 * TAPS
OFFS = 3 * TAPS
TAPS_A_TURN = 3
TURNS = TAPS // TAPS_A_TURN
TR = TAPS_A_TURN * R
ROUND = 1.5 * 2 ** 23

PIECES = ((TCHUNKS - 1,), range(0, 4), range(4, 8))
PLACES = ((0, 0), (0, 1), (1, 0), (1, 1))
COLUMNS = [
    ("ident", P), ("wq0", P), ("wk0", P), ("wv0", R), ("wp0", P), ("ones", 1),
    ("ones0", R), ("dsum", 1),
    ("w1", P), ("bn_g", 3), ("bn_b", 3), ("bn_m", 3), ("bn_v", 3), ("dcn_b", 1),
    ("woff", 4 * R), ("boff", 1), ("osum", OFFS), ("base", TILES * YX), ("w2", TURNS * P), ("w3", P),
    ("wq2", P), ("wk2", P), ("wv2", C), ("bq2", 1), ("bk2", 1), ("bv2", C), ("gamma", 1),
    ("wq3", C), ("wk3", C), ("wvT3", C), ("wp3", C), ("bq3", 1), ("bk3", 1), ("bv3", P), ("bp3", 1),
    ("gn_w", 1), ("gn_b", 1), ("gavg", P),
]
AT, _at = {}, 0
for _name, _width in COLUMNS:
    AT[_name] = (_at, _at + _width)
    _at += _width
WIDTH = _at
FIRST = AT["w1"][0]


def build(nc, x_dram, weights_dram, out_dram):
    fp32, fp32r, bf16, int32 = mybir.dt.float32, mybir.dt.float32r, mybir.dt.bfloat16, mybir.dt.int32
    ALU, ACT, X = mybir.AluOpType, mybir.ActivationFunctionType, mybir.AxisListType.X
    x_view = x_dram.rearrange("b c h w -> b c (h w)")
    out_view = out_dram.rearrange("b c h w -> b c (h w)")
    ctx = ExitStack()
    with ctx:
        def sb(name, shape, dt=fp32):
            return ctx.enter_context(nc.sbuf_tensor(name, shape, dt))

        def sem(name):
            return ctx.enter_context(nc.semaphore(name))

        tables = [nc.dram_tensor(f"cell_table{n}", (TABLE, CORNERS * R), fp32).ap() for n in range(2)]

        wts = sb("wts", [P, WIDTH])

        def wt(name, rows=P):
            a, b = AT[name]
            return wts[0:rows, a:b]

        ident = wt("ident")
        xall = sb("xall", [P, BATCH, N])
        xcur = x2 = sb("xcur_x2", [P, N])
        x3 = sb("x3", [P, N])
        h3 = sb("h3", [P, N])
        q_stack = sb("q_stack", [P, N], fp32r)
        k_stack = sb("k_stack", [P, N], fp32r)
        ident16 = sb("ident16", [P, P], bf16)
        neg_max = sb("neg_max", [P, TILES])
        shift = sb("shift", [P, TILES, R], bf16)
        vT = sb("vT", [P, TILES, C + 1])
        expT = sb("expT", [P, TILES, N])
        inv = sb("inv", [P, TILES])
        oT = sb("oT", [P, TILES, C])
        o4 = oT[:, :, :].rearrange("p t c -> p (t c)")
        h2_stack = sb("h2_stack", [P, N], fp32r)
        w3_stack = sb("w3_stack", [P, P], fp32r)
        bn_std = sb("bn_std", [P, 3])
        bn_s = sb("bn_s", [P, 3])
        bn_t = sb("bn_t", [P, 3])
        cells = sb("cells", [P, CELLS, CELLS])
        tabS = sb("tabS", [P, BATCH, TCHUNKS, P])
        x3s = y = cells[:, :, :].rearrange("p a b -> p (a b)")[:, 0:N]
        h2_full = x2_sum = sb("h2_full_x2_sum", [P, N])
        probsT = sb("probsT", [P, N])
        at = 0
        coordinates = []
        for width in (OFFS, YX, YX, YX, YX, TAPS, TAPS):
            coordinates.append(probsT[:, at:at + TILES * width].rearrange("p (t k) -> p t k", k=width))
            at += TILES * width
        offs, yx, low, frac, rest, mask, mexp = coordinates
        wy = sb("wy", [P, 2, TILES, TAPS])
        rows_all = sb("rows_all", [P, BATCH, TILES * TAPS], int32)
        rows_cur = sb("rows_cur", [P, 2, TILES * TAPS], int32)
        corner_w = sb("corner_w", [P, BATCH, TILES, TAPS * CORNERS])
        got = sb("got", [P, TILES, TAPS, CORNERS * R])
        weighed = sb("weighed", [P, TAPS, CORNERS * R])
        samples = sb("samples", [P, 2, TAPS * R])
        samplesT = sb("samplesT", [TR, TURNS, N])
        stats = sb("stats", [P, 2, 6])
        mom = sb("mom", [P, 2])
        gmom = sb("gmom", [P, 2])
        gsq = sb("gsq", [P, 1])
        gvar = sb("gvar", [P, 1])
        gstd = sb("gstd", [P, 1])
        table_load = sb("table_load", [P, 1])
        gscale = sb("gscale", [P, 1])
        gbias = sb("gbias", [P, 1])
        q3 = offs4 = sb("q3_offs4", [P, N])
        k3 = sb("k3", [P, N])
        v3T = sb("v3T", [P, TILES, C])
        u3 = sb("u3", [P, C])
        bvp3 = sb("bvp3", [P, C])
        bq3s = sb("bq3s", [P, 1])
        bp3s = sb("bp3s", [P, 1])
        neg_max3 = sb("neg_max3", [P, TILES])
        denom3 = sb("denom3", [P, TILES])
        inv3 = sb("inv3", [P, TILES])
        probs = sb("probs", [P, 2, N])
        d4, x1_part = probs[:, 0, :], probs[:, 1, :]
        o3T = h3[:, :].rearrange("p (t c) -> p t c", c=C)

        def pb(name, width):
            return ctx.enter_context(nc.psum_tensor(name, [P, width], fp32))

        xs, xq, ys, yy = pb("xs", N), pb("xq", N), pb("ys", N), pb("yy", N)
        xo, xp = xq[:, 0:HALF], xq[:, HALF:N]
        yo, yt = yy[:, 0:HALF], yy[:, HALF:N]

        weights0_in = sem("weights0_in")
        weights_in = sem("weights_in")
        x_in = [sem(f"x_in{b}") for b in range(BATCH)]
        setup_dve = sem("setup_dve")
        setup_sqrt = sem("setup_sqrt")
        setup_pe = sem("setup_pe")
        setup_act = sem("setup_act")
        x_ready, q_mm, q_high, q_ready, k_mm, k_high, k_ready, v_mm, v_ready = ({
            n: sem(f"{what}_{n}") for n in (0, 2)} for what in (
            "x_ready",
            "q_mm", "q_high", "q_ready",
            "k_mm", "k_high", "k_ready",
            "v_mm", "v_ready"))
        s_mm, max_done, shift_ready, shift_mm, shift_done, t_mm, exp_done, o_mm = ({
            n: sem(f"{what}_{n}") for n in (0, 2)} for what in (
            "s_mm", "max_done",
            "shift_ready", "shift_mm", "shift_done",
            "t_mm", "exp_done",
            "o_mm"))
        inv2_done = sem("inv2_done")
        o_norm = sem("o_norm")
        o_last = sem("o_last")
        ot_mm = sem("ot_mm")
        d4_mm, d4_copied = sem("d4_mm"), sem("d4_copied")
        o4_copied = sem("o4_copied")
        d_mm = sem("d_mm")
        inv0_done = sem("inv0_done")
        inv0_mm = sem("inv0_mm")
        wp_mm = sem("wp_mm")
        wp_copied = sem("wp_copied")
        x1_ready = sem("x1_ready")
        conv1_mm = sem("conv1_mm")
        cells_done = sem("cells_done")
        off4_mm = sem("off4_mm")
        off4_copied = sem("off4_copied")
        off_mm = sem("off_mm")
        off_read = sem("off_read")
        mask_exp = sem("mask_exp")
        rows_ready = sem("rows_ready")
        corner_ready = sem("corner_ready")
        tab_mm = sem("tab_mm")
        tab_copied = sem("tab_copied")
        tab_out = [sem(f"tab_out{n}") for n in range(2)]
        table_free = sem("table_free")
        rows_copied = sem("rows_copied")
        sp_go, pool_go = sem("sp_go"), sem("pool_go")
        got_sem = [sem(f"got{t}") for t in range(TILES)]
        slot_free = sem("slot_free")
        sample_ready = sem("sample_ready")
        st_mm = sem("st_mm")
        st_copied = sem("st_copied")
        w2_mm = sem("w2_mm")
        h2_high = sem("h2_high")
        h2_split = sem("h2_split")
        w3_mm = sem("w3_mm")
        x2_added = sem("x2_added")
        x2_copied = sem("x2_copied")
        mom_ready = sem("mom_ready")
        g_mm = sem("g_mm")
        gvar_ready = sem("gvar_ready")
        gstd_ready = sem("gstd_ready")
        gaff_ready = sem("gaff_ready")
        h3_ready = sem("h3_ready")
        q3_mm = sem("q3_mm")
        q3_ready = sem("q3_ready")
        k3_mm = sem("k3_mm")
        k3_ready = sem("k3_ready")
        v3_mm = sem("v3_mm")
        v3_ready = sem("v3_ready")
        s3_mm = sem("s3_mm")
        max3_done = sem("max3_done")
        exp3_done = sem("exp3_done")
        inv3_done = sem("inv3_done")
        pt_mm = sem("pt_mm")
        pt_dve = sem("pt_dve")
        pt_act = sem("pt_act")
        o3_mm = sem("o3_mm")
        o3_norm = sem("o3_norm")
        ot3_mm = sem("ot3_mm")
        y_ready = sem("y_ready")
        y_out = sem("y_out")

        block = ctx.enter_context(nc.Block())

        def halves(bank):
            return [(bank[:, h * HALF:(h + 1) * HALF], slice(h * HALF, (h + 1) * HALF)) for h in range(2)]

        def quarter(c, n=1):
            return slice(c * R, (c + n) * R)

        @block.sync
        def _(sp):
            sp.dma_start(wts[:, 0:FIRST], weights_dram[:, 0:FIRST]).then_inc(weights0_in, 16)
            for b in range(1, BATCH):
                sp.dma_start(xall[:, b, :], x_view[b]).then_inc(x_in[b], 16)
            tab_pair = tabS[:, :, :, :].rearrange("p (a n) k d -> p a n k d", n=2)
            with sp.Fori(0, BATCH // 2) as i:
                for n, table in enumerate(tables):
                    sp.wait_ge(tab_copied, 6 * i + 3 * n + 3)
                    sp.sem_inc(sp_go, 1)
                    sp.wait_ge(table_free, 2 * i + n + 1)
                    sp.sem_inc(sp_go, 1)
                    sp.dma_start(table[0:(TCHUNKS - 1) * P, :].rearrange("(k p) d -> p k d", p=P),
                                 tab_pair[:, bass.ds(i, 1), n, 0:TCHUNKS - 1, :].rearrange("p a k d -> p (a k) d"))\
                        .then_inc(tab_out[n], 16)
                    sp.dma_start(table[(TCHUNKS - 1) * P:TABLE, :],
                                 tab_pair[0:TLAST, bass.ds(i, 1), n, TCHUNKS - 1, :].rearrange("p a d -> p (a d)"))\
                        .then_inc(tab_out[n], 16)
            with sp.Fori(0, BATCH - 1) as i:
                sp.wait_ge(y_ready, i + 2)
                sp.sem_inc(sp_go, 1)
                sp.dma_start(out_view[bass.ds(i, 1), :, :].rearrange("b c n -> (b c) n"), y[:, :]).then_inc(y_out, 16)
            for h in range(2):
                at = slice(h * HALF, (h + 1) * HALF)
                sp.wait_ge(y_ready, BATCH + 1 + h)
                sp.dma_start(out_view[BATCH - 1, :, at], y[:, at]).then_inc(y_out, 16)
            sp.wait_ge(y_out, 16 + 16 * (BATCH + 1))
            for n in range(2):
                sp.wait_ge(tab_out[n], 16 * BATCH)

        @block.gpsimd
        def _(pool):
            rows_pair = rows_all[:, :, :].rearrange("p (a n) k -> p a n k", n=2)
            with pool.Fori(0, BATCH // 2) as i:
                for n, table in enumerate(tables):
                    pool.wait_ge(rows_ready, 2 * i + n + 1)
                    nc.gpsimd.tensor_copy(rows_cur[:, n, :],
                                          rows_pair[:, bass.ds(i, 1), n, :].rearrange("p a k -> p (a k)"))\
                        .then_inc(rows_copied, 1)
                    pool.wait_ge(rows_copied, 2 * i + n + 1)
                    pool.wait_ge(tab_out[n], 32 * i + 32)
                    for t in range(TILES):
                        pool.wait_ge(slot_free, 2 * TILES * i + TILES * n + t + 1)
                        pool.sem_inc(pool_go, 1)
                        for k in range(TAPS):
                            at = t * TAPS + k
                            nc.gpsimd.indirect_dma_start(
                                got[:, t, k, :], None, table,
                                bass.IndirectOffsetOnAxis(ap=rows_cur[:, n, at:at + 1], axis=0)).then_inc(got_sem[t], 16)

        @block.tensor
        def _(pe):
            def project(to, w, x, done):
                for bank, at in halves(to):
                    last = nc.tensor.matmul(bank, w, x[:, at], start=True, stop=True)
                last.then_inc(done, 1)

            def scores(L, i, t, bank):
                for to, at in halves(bank):
                    last = nc.tensor.matmul(to, q_stack[0:3 * R, t * P:(t + 1) * P], k_stack[0:3 * R, at],
                                            start=True, stop=True)
                last.then_inc(s_mm[L], 1)

            def shift_rows(L, i, bank):
                pe.wait_ge(shift_ready[L], i + 1)
                for t in range(TILES):
                    last = nc.tensor.matmul(bank[3 * R:4 * R, t * P:(t + 1) * P], shift[:, t, :], ident16[:, :],
                                            start=True, stop=True)
                last.then_inc(shift_mm[L], 1)

            def shifted_scores(L, i, j, bank):
                for to, at in halves(bank):
                    last = nc.tensor.matmul(to, k_stack[:, j * P:(j + 1) * P], q_stack[:, at], start=True, stop=True)
                last.then_inc(t_mm[L], 1)

            def weigh_values(L, t, to, width):
                for j in range(TILES):
                    last = nc.tensor.matmul(to, expT[:, j, t * P:(t + 1) * P], vT[:, j, C - width:C + 1],
                                            start=j == 0, stop=j == TILES - 1)
                last.then_inc(o_mm[L], 1)

            def l0_project(i):
                pe.wait_ge(x_ready[0], i + 1)
                project(xq, wt("wq0"), xcur, q_mm[0])
                project(yy, wt("wk0"), xcur, k_mm[0])

            def l0_values_in(i, h):
                for j in range(h * TILES // 2, (h + 1) * TILES // 2):
                    last = nc.tensor.matmul(xo[:, j * R:(j + 1) * R], xcur[:, j * P:(j + 1) * P], wt("wv0"),
                                            start=True, stop=True)
                if h:
                    last.then_inc(v_mm[0], 1)

            def l0_scores(i, t):
                if t == 0:
                    pe.wait_ge(q_ready[0], i + 1)
                    pe.wait_ge(k_ready[0], i + 1)
                if t >= 2:
                    pe.wait_ge(max_done[0], TILES * i + t - 1)
                scores(0, i, t, (xs, ys)[t % 2])

            def l0_shift(i):
                pe.wait_ge(max_done[0], TILES * i + TILES - 1)
                shift_rows(0, i, xs)

            def l0_shifted(i, j):
                if j == 0:
                    pe.wait_ge(shift_done[0], i + 1)
                    pe.wait_ge(max_done[0], TILES * i + TILES)
                if j >= 2:
                    pe.wait_ge(exp_done[0], TILES * i + j - 1)
                shifted_scores(0, i, j, (ys, xs)[j % 2])

            def l0_parts(to, g, v):
                for bank, at in halves(to):
                    for c in range(4):
                        j = g * 4 + c
                        last = nc.tensor.matmul(bank[quarter(c), :], v(j), expT[:, j, at],
                                                start=g == 0, stop=g == TILES // 4 - 1)
                return last

            def l0_denominators(i, g, pair):
                pe.wait_ge(exp_done[0], TILES * i + (TILES if g else TILES - 1 if pair is ys else TILES // 2))
                last = l0_parts(pair, g, lambda j: wt("ones0"))
                if g:
                    last.then_inc(d4_mm, 1)

            def l0_values(i):
                l0_parts(xs, 0, lambda j: vT[:, j, C - R:C])
                l0_parts(xs, 1, lambda j: vT[:, j, C - R:C]).then_inc(o_mm[0], 1)

            def l0_end(i, samples_too):
                pe.wait_ge(d4_copied, i + 1)
                for t in range(TILES):
                    last = nc.tensor.matmul(ys[:, t:t + 1], d4[:, t * P:(t + 1) * P], wt("dsum"), start=True, stop=True)
                last.then_inc(d_mm, 1)
                pe.wait_ge(o4_copied, i + 1)
                project(xs, wt("wp0"), o4, wp_mm)
                if samples_too:
                    l1_turn(0, 2, xo)
                pe.wait_ge(inv0_done, i + 1)
                for t in range(TILES):
                    last = nc.tensor.matmul(ys[:, t * P:(t + 1) * P], inv[:, t:t + 1].to_broadcast([P, P]), ident,
                                            start=True, stop=True)
                last.then_inc(inv0_mm, 1)
                if samples_too:
                    l1_turn(0, 3, xo)

            def l1_conv1(i, h, bank, pieces=(0, 1)):
                for piece in pieces:
                    at = piece * HALF // 2
                    last = nc.tensor.matmul(bank[:, at:at + HALF // 2], wt("w1"),
                                            xall[:, bass.ds(i, 1), h * HALF + at:h * HALF + at + HALF // 2]
                                            .rearrange("p b n -> p (b n)"), start=True, stop=True)
                if 1 in pieces:
                    last.then_inc(conv1_mm, 1)

            def l1_offsets(i, h):
                pe.wait_ge(cells_done, 2 * CORNERS * i + 2 * CORNERS)
                for n, (a, b) in enumerate(PLACES):
                    last = nc.tensor.matmul((yt, yo)[h][quarter(n), :], wt("woff")[:, quarter(n)],
                                            cells[:, h * H // 2 + a:(h + 1) * H // 2 + a, b:b + W],
                                            start=True, stop=True)
                last.then_inc(off4_mm, 1)

            def l1_offsets_turn(i, part, bank):
                if part == 0:
                    pe.wait_ge(off4_copied, 2 * i + 2)
                for t in range(2 * part, 2 * part + 2):
                    last = nc.tensor.matmul(bank[:, t * OFFS:(t + 1) * OFFS], offs4[:, t * P:(t + 1) * P], wt("osum"),
                                            start=True, stop=True)
                if part == 3:
                    last.then_inc(off_mm, 1)

            def l1_table(i, n, bank):
                flat = cells[:, :, :].rearrange("p a b -> p (a b)")
                for k in PIECES[n]:
                    rows = P if k < TCHUNKS - 1 else TLAST
                    last = nc.tensor.transpose(bank[0:rows, k % 4 * P:(k % 4 + 1) * P],
                                               flat[:, k * P:k * P + rows], ident)
                last.then_inc(tab_mm, 1)

            def l1_turn(i, t, bank):
                pe.wait_ge(sample_ready, TILES * i + t + 1)
                if t:
                    pe.wait_ge(st_copied, TILES * i + t)
                for g in range(TURNS):
                    last = nc.tensor.transpose(bank[0:TR, g * P:(g + 1) * P],
                                               samples[:, t % 2, g * TR:(g + 1) * TR], ident)
                last.then_inc(st_mm, 1)

            def l1_conv2(i, h):
                pe.wait_ge(st_copied, TILES * i + (TILES // 2) * (h + 1))
                bank, at = halves(ys)[h]
                for g in range(TURNS):
                    last = nc.tensor.matmul(bank, wt("w2", TR)[:, g * P:(g + 1) * P], samplesT[:, g, at],
                                            start=g == 0, stop=g == TURNS - 1)
                if h:
                    last.then_inc(w2_mm, 1)

            def l1_conv3(i):
                pe.wait_ge(h2_split, i + 1)
                project(ys, w3_stack[:, :], h2_stack, w3_mm)

            def l2_q(i):
                pe.wait_ge(x_ready[2], i + 1)
                project(ys, wt("wq2"), x2, q_mm[2])

            def l2_k(i):
                project(xq, wt("wk2"), x2, k_mm[2])

            def l2_v(i):
                for j in range(TILES):
                    last = nc.tensor.matmul(xs[:, j * C:(j + 1) * C], x2[:, j * P:(j + 1) * P], wt("wv2"),
                                            start=True, stop=True)
                last.then_inc(v_mm[2], 1)

            def l2_scores(i, t):
                if t == 0:
                    pe.wait_ge(q_ready[2], i + 1)
                    pe.wait_ge(k_ready[2], i + 1)
                if t >= 2:
                    pe.wait_ge(max_done[2], TILES * i + t - 1)
                scores(2, i, t, (xq, xs)[t % 2])

            def l2_shifted(i, j):
                if j == 0:
                    pe.wait_ge(shift_done[2], i + 1)
                if j >= 2:
                    pe.wait_ge(exp_done[2], TILES * i + j - 1)
                shifted_scores(2, i, j, (xs, xq)[j % 2])

            def l2_values(i, t):
                if t == 0:
                    pe.wait_ge(exp_done[2], TILES * i + TILES)
                if t >= 2:
                    pe.wait_ge(o_norm, (TILES - 1) * i + t - 1)
                weigh_values(2, t, (xo, xp)[t % 2][:, 0:C + 1], C)

            def l2_end(i, h):
                for t in range(h * TILES // 2, (h + 1) * TILES // 2):
                    if t < TILES - 1:
                        pe.wait_ge(o_norm, (TILES - 1) * i + t + 1)
                    else:
                        pe.wait_ge(o_last, i + 1)
                    last = nc.tensor.transpose(xs[:, t * P:(t + 1) * P], oT[:, t, :], ident)
                last.then_inc(ot_mm, 1)

            def l3_groups(i):
                pe.wait_ge(mom_ready, i + 1)
                nc.tensor.matmul(yo[:, 0:2], wt("gavg"), mom[:, :], start=True, stop=True).then_inc(g_mm, 1)

            def l3_project(i):
                pe.wait_ge(h3_ready, 2 * i + 1)
                project(yy, wt("wq3"), h3, q3_mm)

            def l3_k(i):
                project(ys, wt("wk3"), h3, k3_mm)

            def l3_values_in(i, h):
                if h == 0:
                    pe.wait_ge(q3_ready, i + 1)
                for j in range(h * TILES // 2, (h + 1) * TILES // 2):
                    last = nc.tensor.matmul(yy[:, j * C:(j + 1) * C], h3[:, j * P:(j + 1) * P], u3[:, :],
                                            start=True, stop=True)
                if h:
                    last.then_inc(v3_mm, 1)

            def l3_scores(i, t, pair):
                if t == 0:
                    pe.wait_ge(k3_ready, i + 1)
                for to, at in halves(pair):
                    last = nc.tensor.matmul(to, q3[:, t * P:(t + 1) * P], k3[:, at], start=True, stop=True)
                last.then_inc(s3_mm, 1)

            def l3_turn(i, t, h, bank):
                if h and bank is yt:
                    pe.wait_ge(pt_dve, TILES * i + t + 1)
                elif not h:
                    pe.wait_ge(exp3_done, TILES * i + t + 1)
                    if t == 0:
                        pe.wait_ge(v3_ready, i + 1)
                for j in range(TILES // 2):
                    at = (h * TILES // 2 + j) * P
                    last = nc.tensor.transpose(bank[:, j * P:(j + 1) * P], probs[:, t % 2, at:at + P], ident)
                last.then_inc(pt_mm, 1)

            def l3_values(i, t):
                pe.wait_ge(pt_act, TILES * i + t + 1)
                pe.wait_ge(pt_dve, TILES * i + t + 1)
                if t:
                    pe.wait_ge(o3_norm, TILES * i + t)
                for j in range(TILES):
                    last = nc.tensor.matmul(yo[:, 0:C], probsT[:, j * P:(j + 1) * P], v3T[:, j, :],
                                            start=j == 0, stop=j == TILES - 1)
                last.then_inc(o3_mm, 1)

            def l3_end(i, first, end):
                pe.wait_ge(o3_norm, TILES * i + end)
                for t in range(first, end):
                    last = nc.tensor.transpose(ys[:, t * P:(t + 1) * P], o3T[:, t, :], ident)
                last.then_inc(ot3_mm, 1)

            def first_loop_step(a, b, following, samples_too=False):
                if b is not None:
                    pe.wait_ge(x1_ready, b + 1)
                    pe.wait_ge(q_ready[0], a + 1)
                    l1_conv1(b, 0, xp)
                for t in range(TILES):
                    l0_scores(a, t)
                    if t in (4, 5):
                        l0_values_in(a, t - 4)
                    if b is not None and t in (1, 2):
                        l1_conv1(b, 1, yo, (t - 1,))
                    if b is not None and t == 6:
                        l1_offsets(b, 0)
                if b is not None:
                    l1_offsets(b, 1)
                l0_shift(a)
                if b is not None:
                    l1_offsets_turn(b, 0, xp)
                    l1_offsets_turn(b, 1, xp)
                    l1_offsets_turn(b, 2, xp)
                for j in range(TILES):
                    l0_shifted(a, j)
                    if b is not None and j == 1:
                        l1_offsets_turn(b, 3, xp)
                    if b is not None and j == 4:
                        pe.wait_ge(v_ready[0], a + 1)
                        l1_table(b, 0, xo)
                    if b is not None and j in (5, 6):
                        l1_table(b, j - 4, (yt, yo)[j - 5])
                pe.wait_ge(v_ready[0], a + 1)
                if b is not None:
                    pe.wait_ge(off_read, b + 1)
                    pe.wait_ge(tab_copied, 3 * b + 1)
                for g in range(2):
                    l0_denominators(a, g, ys if samples_too else xq)
                if samples_too:
                    l1_turn(0, 0, xo)
                l0_values(a)
                if samples_too:
                    l1_turn(0, 1, xo)
                l0_end(a, samples_too)
                if b is not None:
                    pe.wait_ge(tab_copied, 3 * b + 3)
                if following is not None:
                    l0_project(following)

            def second_loop_step(a, b, c):
                L3, L2, SAMPLES = a is not None, b is not None, c is not None
                turn_banks = (yt, yt) if L2 else (yt, xp)
                if L2:
                    l2_q(b)
                if L3:
                    l3_groups(a)
                if L2:
                    if not L3:
                        pe.wait_ge(off_read, BATCH)
                    l2_k(b)
                    l2_v(b)
                if L3:
                    l3_project(a)
                    if L2:
                        pe.wait_ge(q_ready[2], b + 1)
                    l3_k(a)
                    l3_values_in(a, 0)
                if SAMPLES and not L3:
                    pe.wait_ge(off4_copied, 2 * BATCH)
                    l1_turn(c, 0, yo)
                    l1_turn(c, 1, yo)
                if L3:
                    l3_scores(a, 0, ys)
                    l3_values_in(a, 1)
                if L2:
                    l2_scores(b, 0)
                    pe.wait_ge(v_ready[2], b + 1)
                    l2_scores(b, 1)
                start = 4 if L3 else 2
                for t in range(TILES):
                    if L2 and not L3 and t == 3:
                        pe.wait_ge(tab_copied, 3 * BATCH)
                    if L3:
                        if not L2 and t == 0:
                            l3_scores(a, 1, xs)
                        l3_turn(a, t, 0, turn_banks[0])
                    if L3 and L2 and t == TILES - 1:
                        l2_values(b, 0)
                    if L2 and t == 3:
                        shift_rows(2, b, xq)
                    if L3 and L2 and t + 1 < TILES:
                        l3_scores(a, t + 1, ys)
                    if SAMPLES and t > 3:
                        if L3:
                            pe.wait_ge(o3_norm, TILES * a + t)
                        l1_turn(c, t - start, yo)
                    if L3:
                        l3_turn(a, t, 1, turn_banks[1])
                    if L3 and not L2 and t + 2 < TILES:
                        l3_scores(a, t + 2, (ys, xs)[t % 2])
                    if L2:
                        for n in (2 * t, 2 * t + 1):
                            if not L3 and n == 4:
                                pe.wait_ge(q_ready[2], b + 1)
                                pe.wait_ge(st_copied, TILES * c + 2)
                                for piece, bank in enumerate((ys, yt, yo)):
                                    l1_table(BATCH - 1, piece, bank)
                            if t < 3:
                                l2_scores(b, n + 2)
                            elif t < 7:
                                l2_shifted(b, n - 6)
                            elif not L3 or n == 15:
                                l2_values(b, n - 14)
                    if SAMPLES and t > 3:
                        pe.wait_ge(st_copied, TILES * c + t - start + 1)
                    if L3 and not L2 and t == TILES - 1:
                        l3_end(a, 0, TILES // 2)
                    if L3:
                        l3_values(a, t)
                if SAMPLES:
                    l1_turn(c, TILES - start, yt)
                if L3:
                    if L2 and not SAMPLES:
                        l2_values(b, 2)
                    l3_end(a, 0 if L2 else TILES // 2, TILES)
                    if SAMPLES:
                        l1_turn(c, 5, yt)
                if L3 or not SAMPLES:
                    if L2:
                        for n in range(2 if SAMPLES else 3, TILES):
                            l2_values(b, n)
                            if SAMPLES and n == 4:
                                l1_turn(c, 6, yt)
                                pe.wait_ge(y_ready, a + 2)
                                l1_conv2(c, 0)
                                l1_turn(c, 7, yt)
                                l1_conv2(c, 1)
                            if SAMPLES and n == 6:
                                l1_conv3(c)
                            if n == 6:
                                l2_end(b, 0)
                        l2_end(b, 1)
                else:
                    for n in range(2, TILES):
                        l2_values(b, n)
                        if n == 2:
                            l1_conv2(c, 0)
                        if n == 3:
                            l1_turn(c, 7, yt)
                            l1_conv2(c, 1)
                        if n == 6:
                            l1_conv3(c)
                            l2_end(b, 0)
                    l2_end(b, 1)

            pe.wait_ge(weights0_in, 16)
            l0_project(0)
            first_loop_step(0, None, 1)
            pe.wait_ge(weights_in, 16)
            with pe.Fori(0, BATCH - 2) as i:
                first_loop_step(i + 1, i, i + 2)
            first_loop_step(BATCH - 1, BATCH - 2, None, samples_too=True)
            l1_turn(0, 4, xo)
            pe.wait_ge(x1_ready, BATCH)
            l1_conv1(BATCH - 1, 0, yt)
            nc.tensor.matmul(ys[:, 0:C], wt("wvT3"), wt("wp3"), start=True, stop=True)
            nc.tensor.matmul(ys[:, C:2 * C], wt("bv3"), wt("wp3"), start=True, stop=True).then_inc(setup_pe, 1)
            l1_turn(0, 5, xo)
            l1_conv1(BATCH - 1, 1, yo)
            l1_turn(0, 6, xo)
            pe.wait_ge(setup_act, 2)
            l1_conv2(0, 0)
            l1_turn(0, 7, xo)
            l1_conv2(0, 1)
            for h in range(2):
                l1_offsets(BATCH - 1, h)
            l1_conv3(0)
            for part in range(4):
                l1_offsets_turn(BATCH - 1, part, xp)
            second_loop_step(None, 0, 1)
            with pe.Fori(0, BATCH - 2) as i:
                second_loop_step(i, i + 1, i + 2)
            second_loop_step(BATCH - 2, BATCH - 1, None)
            second_loop_step(BATCH - 1, None, None)

        @block.scalar
        def _(act):
            def copy(to, bank):
                return nc.scalar.activation(to, bank, ACT.Copy)

            def exponentials(L, i, j, bank):
                act.wait_ge(t_mm[L], TILES * i + j + 1)
                nc.scalar.activation(expT[:, j, :], bank[:, :], ACT.Exp).then_inc(exp_done[L], 1)

            def shift_copy(L, i, bank):
                act.wait_ge(shift_mm[L], i + 1)
                copy(q_stack[quarter(3), :], bank[quarter(3), :]).then_inc(shift_done[L], 1)

            def l0_project(i):
                act.wait_ge(q_mm[0], i + 1)
                nc.scalar.activation(q_stack[0:3 * R, :], xq[0:3 * R, :], ACT.Copy, scale=float(R) ** -0.5)\
                    .then_inc(q_high[0], 1)
                act.wait_ge(k_mm[0], i + 1)
                copy(k_stack[0:3 * R, :], yy[0:3 * R, :]).then_inc(k_high[0], 1)

            def l0_values_in(i):
                act.wait_ge(v_mm[0], i + 1)
                copy(vT[:, :, C - R:C], xo[:, 0:TILES * R].rearrange("p (j r) -> p j r", r=R)).then_inc(v_ready[0], 1)

            def l0_end(i):
                act.wait_ge(o_mm[0], i + 1)
                copy(o4, xs[:, :]).then_inc(o4_copied, 1)

            def l0_projected(i):
                act.wait_ge(wp_mm, i + 1)
                copy(x1_part, xs[:, :]).then_inc(wp_copied, 1)

            def l0_next(i):
                copy(xcur[:, :], xall[:, bass.ds(i, 1), :].rearrange("p b n -> p (b n)")).then_inc(x_ready[0], 1)

            def l1_cells(i, h, bank):
                act.wait_ge(conv1_mm, 2 * i + h + 1)
                for c in range(CORNERS):
                    dy, dx = c // 2, c % 2
                    at = slice(1 - dy + h * H // 2, 1 - dy + (h + 1) * H // 2)
                    nc.scalar.activation(cells[quarter(c), at, 1 - dx:1 - dx + W],
                                         bank[quarter(c), :].rearrange("p (a b) -> p a b", b=W), ACT.Relu,
                                         bias=bn_t[quarter(c), 0:1], scale=bn_s[quarter(c), 0:1]).then_inc(cells_done, 1)

            def l1_offsets(i, h):
                act.wait_ge(off4_mm, 2 * i + h + 1)
                nc.scalar.activation(offs4[:, h * HALF:(h + 1) * HALF], (yt, yo)[h][:, :], ACT.Identity,
                                     bias=wt("boff")).then_inc(off4_copied, 1)

            def l1_mask(i):
                act.wait_ge(off_read, i + 1)
                nc.scalar.activation(mexp[:, :, :], offs[:, :, YX:OFFS], ACT.Exp, scale=-1.0).then_inc(mask_exp, 1)

            def l1_table(i, n, bank):
                act.wait_ge(tab_mm, 3 * i + n + 1)
                first, chunks = PIECES[n][0], len(PIECES[n])
                rows = P if first < TCHUNKS - 1 else TLAST
                to = tabS[0:rows, bass.ds(i, 1), first:first + chunks, :].rearrange("p i k d -> p (i k) d")
                copy(to, bank[0:rows, 0:chunks * P].rearrange("p (k d) -> p k d", d=P)).then_inc(tab_copied, 1)

            def l1_turn(i, t, bank):
                act.wait_ge(st_mm, TILES * i + t + 1)
                copy(samplesT[:, :, t * P:(t + 1) * P],
                     bank[0:TR, 0:TURNS * P].rearrange("p (g n) -> p g n", g=TURNS)).then_inc(st_copied, 1)

            def l1_conv2(i):
                act.wait_ge(w2_mm, i + 1)
                for to in (h2_full, h2_stack):
                    nc.scalar.activation(to[:, :], ys[:, :], ACT.Relu, bias=bn_t[:, 1:2], scale=bn_s[:, 1:2])\
                        .then_inc(h2_high, 1)

            def l1_end(i):
                act.wait_ge(x2_added, i + 1)
                nc.scalar.activation(x2[:, :], x2_sum[:, :], ACT.Relu, bias=bn_t[:, 2:3]).then_inc(x_ready[2], 1)

            def l1_keep(i):
                copy(xall[:, bass.ds(i, 1), :].rearrange("p b n -> p (b n)"), x2[:, :]).then_inc(x2_copied, 1)

            def l2_q(i):
                act.wait_ge(q_mm[2], i + 1)
                nc.scalar.activation(q_stack[0:3 * R, :], ys[0:3 * R, :], ACT.Identity, bias=wt("bq2")[0:3 * R, :])\
                    .then_inc(q_high[2], 1)

            def l2_k(i):
                act.wait_ge(k_mm[2], i + 1)
                nc.scalar.activation(k_stack[0:3 * R, :], xq[0:3 * R, :], ACT.Identity, bias=wt("bk2")[0:3 * R, :])\
                    .then_inc(k_high[2], 1)

            def l2_values(i, t):
                act.wait_ge(inv2_done, TILES * i + t + 1)
                nc.scalar.activation(oT[:, t, :], (xo, xp)[t % 2][:, 0:C], ACT.Copy, scale=inv[:, t:t + 1])\
                    .then_inc(o_norm, 1)

            def l3_deviation(i):
                act.wait_ge(gvar_ready, i + 1)
                nc.scalar.activation(gstd[:, :], gvar[:, :], ACT.Sqrt).then_inc(gstd_ready, 1)

            def l3_norm(i):
                act.wait_ge(gaff_ready, i + 1)
                nc.scalar.activation(h3[:, :], x3[:, :], ACT.Identity, bias=gbias[:, :], scale=gscale[:, :])\
                    .then_inc(h3_ready, 1)

            def l3_residual(i):
                act.wait_ge(y_out, 16 * i + 16)
                nc.scalar.activation(x3s[:, :], x3[:, :], ACT.Identity, bias=bp3s[:, :], scale=2.0 ** -0.5)\
                    .then_inc(h3_ready, 1)

            def l3_q(i):
                act.wait_ge(q3_mm, i + 1)
                nc.scalar.activation(q3[:, :], yy[:, :], ACT.Identity, bias=bq3s[:, :], scale=float(C) ** -0.5)\
                    .then_inc(q3_ready, 1)

            def l3_k(i):
                act.wait_ge(k3_mm, i + 1)
                nc.scalar.activation(k3[:, :], ys[:, :], ACT.Identity, bias=wt("bk3")).then_inc(k3_ready, 1)

            def l3_exp(i, t, pair):
                act.wait_ge(max3_done, TILES * i + t + 1)
                if t >= 2:
                    act.wait_ge(pt_mm, 2 * TILES * i + 2 * (t - 1))
                nc.scalar.activation(probs[:, t % 2, :], pair[:, :], ACT.Exp, bias=neg_max3[:, t:t + 1],
                                     accum_out=denom3[:, t:t + 1]).then_inc(exp3_done, 1)

            def l3_turn(i, t, bank):
                act.wait_ge(pt_mm, 2 * TILES * i + 2 * t + 2)
                copy(probsT[:, HALF:N], bank[:, :]).then_inc(pt_act, 1)

            def l3_values(i, t):
                act.wait_ge(o3_mm, TILES * i + t + 1)
                act.wait_ge(inv3_done, TILES * i + t + 1)
                nc.scalar.activation(o3T[:, t, :], yo[:, 0:C], ACT.Copy, scale=inv3[:, t:t + 1]).then_inc(o3_norm, 1)

            def first_loop_step(a, b, following, samples_too=False):
                if b is not None:
                    l1_cells(b, 0, xp)
                    l1_cells(b, 1, yo)
                l0_values_in(a)
                if b is not None:
                    for h in range(2):
                        l1_offsets(b, h)
                shift_copy(0, a, xs)
                for j in range(TILES):
                    exponentials(0, a, j, (ys, xs)[j % 2])
                    if b is not None and j == 5:
                        l1_mask(b)
                        l1_table(b, 0, xo)
                if b is not None:
                    l1_table(b, 1, yt)
                    l1_table(b, 2, yo)
                if samples_too:
                    l1_turn(0, 0, xo)
                if following is not None:
                    l0_next(following)
                l0_end(a)
                if samples_too:
                    l1_turn(0, 1, xo)
                l0_projected(a)
                if samples_too:
                    l1_turn(0, 2, xo)
                    l1_turn(0, 3, xo)
                if following is not None:
                    l0_project(following)

            def second_loop_step(a, b, c):
                L3, L2, SAMPLES = a is not None, b is not None, c is not None
                if L3:
                    nc.scalar.activation(table_load[:, :], wt("ones0")[:, 0:1], ACT.Sqrt)
                if L2:
                    l2_q(b)
                if L3:
                    l3_deviation(a)
                    l3_norm(a)
                if L2:
                    l2_k(b)
                if L3:
                    l3_q(a)
                    l3_k(a)
                if L2:
                    l1_keep(b)
                if L3:
                    l3_residual(a)
                    l3_exp(a, 0, ys)
                if SAMPLES and not L3:
                    l1_turn(c, 0, yo)
                    l1_turn(c, 1, yo)
                start = 4 if L3 else 2
                for t in range(TILES):
                    if L3 and t:
                        l3_values(a, t - 1)
                    if L2 and not L3 and t == 2:
                        for piece, bank in enumerate((ys, yt, yo)):
                            l1_table(BATCH - 1, piece, bank)
                    if L2 and t == 3:
                        shift_copy(2, b, xq)
                    if SAMPLES and t > 3:
                        l1_turn(c, t - start, yo)
                    if L3:
                        l3_turn(a, t, yt if L2 else xp)
                    if L2 and 3 <= t < 7:
                        exponentials(2, b, 2 * t - 6, xs)
                    if L3 and t + 1 < TILES:
                        l3_exp(a, t + 1, (ys if L2 else (ys, xs)[(t + 1) % 2]))
                    if L2 and 3 <= t < 7:
                        exponentials(2, b, 2 * t - 5, xq)
                if L2:
                    l2_values(b, 0)
                    l2_values(b, 1)
                if L3:
                    l3_values(a, TILES - 1)
                if SAMPLES:
                    l1_turn(c, TILES - start, yt)
                if L3 and SAMPLES:
                    l1_turn(c, 5, yt)
                if L2:
                    for n in range(2, TILES - 1):
                        l2_values(b, n)
                        if SAMPLES and L3 and n == 4:
                            l1_turn(c, 6, yt)
                            l1_turn(c, 7, yt)
                            l1_conv2(c)
                        if SAMPLES and not L3 and n == 3:
                            l1_turn(c, 7, yt)
                        if SAMPLES and not L3 and n == 4:
                            l1_conv2(c)
                if SAMPLES:
                    l1_end(c)

            act.dma_start(xall[:, 0, :], x_view[0]).then_inc(x_in[0], 16)
            act.dma_start(wts[:, FIRST:WIDTH], weights_dram[:, FIRST:WIDTH]).then_inc(weights_in, 16)
            act.wait_ge(weights0_in, 16)
            l0_project(0)
            act.wait_ge(x_in[1], 16)
            first_loop_step(0, None, 1)
            act.wait_ge(setup_dve, 1)
            nc.scalar.activation(bn_std[:, :], bn_std[:, :], ACT.Sqrt).then_inc(setup_sqrt, 1)
            act.wait_ge(setup_dve, 2)
            for b in range(2, BATCH):
                act.wait_ge(x_in[b], 16)
            with act.Fori(0, BATCH - 2) as i:
                first_loop_step(i + 1, i, i + 2)
            first_loop_step(BATCH - 1, BATCH - 2, None, samples_too=True)
            l1_turn(0, 4, xo)
            l1_cells(BATCH - 1, 0, yt)
            act.wait_ge(setup_pe, 1)
            for n, to in enumerate((u3, bvp3)):
                copy(to[:, :], ys[:, n * C:(n + 1) * C]).then_inc(setup_act, 1)
            l1_turn(0, 5, xo)
            l1_turn(0, 6, xo)
            l1_cells(BATCH - 1, 1, yo)
            l1_turn(0, 7, xo)
            l1_conv2(0)
            for h in range(2):
                l1_offsets(BATCH - 1, h)
            l1_end(0)
            l1_mask(BATCH - 1)
            second_loop_step(None, 0, 1)
            with act.Fori(0, BATCH - 2) as i:
                second_loop_step(i, i + 1, i + 2)
            second_loop_step(BATCH - 2, BATCH - 1, None)
            second_loop_step(BATCH - 1, None, None)

        @block.vector
        def _(dve):
            def low_part(stack, c, bank, n, before, high, done, op=ALU.add):
                dve.wait_ge(high, n)
                nc.vector.scalar_tensor_tensor(stack[quarter(c), :], bank[quarter(c), :], before,
                                               stack[quarter(c), :].bitcast(fp32), op, ALU.subtract).then_inc(done, 1)

            def maximum(L, i, t, bank):
                dve.wait_ge(s_mm[L], TILES * i + t + 1)
                nc.vector.tensor_reduce(neg_max[:, t:t + 1], bank[:, :], axis=X, op=ALU.max,
                                        negate=True).then_inc(max_done[L], 1)

            def shift_parts(L, i):
                dve.drain()
                nc.vector.tensor_copy(shift[:, :, 0:1], neg_max[:, :].rearrange("p (t a) -> p t a", a=1))
                dve.drain()
                nc.vector.tensor_tensor(shift[:, :, 1:2], neg_max[:, :].rearrange("p (t a) -> p t a", a=1),
                                        shift[:, :, 0:1], ALU.subtract).then_inc(shift_ready[L], 1)

            def l0_project(i):
                low_part(q_stack, 2, xq, i + 1, float(R) ** -0.5, q_high[0], q_ready[0], ALU.mult)
                low_part(k_stack, 1, yy, i + 1, 0.0, k_high[0], k_ready[0])

            def l0_denominators(i, samples_too):
                if samples_too:
                    l1_samples(0, 0)
                dve.wait_ge(d4_mm, i + 1)
                nc.vector.tensor_copy(d4, (ys if samples_too else xq)[:, :]).then_inc(d4_copied, 1)
                if samples_too:
                    l1_samples(0, 1)
                    l1_samples(0, 2)
                dve.wait_ge(d_mm, i + 1)
                nc.vector.reciprocal(inv[:, :], ys[:, 0:TILES]).then_inc(inv0_done, 1)
                if samples_too:
                    l1_samples(0, 3)

            def l0_end(i):
                dve.wait_ge(inv0_mm, i + 1)
                dve.wait_ge(wp_copied, i + 1)
                nc.vector.tensor_tensor(x1_part, ys[:, :], x1_part, ALU.mult)
                dve.drain()
                x = xall[:, bass.ds(i, 1), :].rearrange("p b n -> p (b n)")
                nc.vector.tensor_tensor(x, x1_part, x, ALU.add).then_inc(x1_ready, 1)

            def l1_coordinates(i, bank):
                dve.wait_ge(off_mm, i + 1)
                nc.vector.tensor_copy(offs[:, :, :], bank[:, 0:TILES * OFFS].rearrange("p (t k) -> p t k", k=OFFS))\
                    .then_inc(off_read, 1)
                dve.drain()
                nc.vector.tensor_tensor(yx[:, :, :], offs[:, :, 0:YX],
                                        wt("base").rearrange("p (t k) -> p t k", k=YX), ALU.add)
                dve.drain()
                nc.vector.tensor_scalar(yx[:, :, :], yx[:, :, :], -1.0, float(H), ALU.max, ALU.min)
                dve.drain()
                nc.vector.tensor_scalar(low[:, :, :], yx[:, :, :], 0.5, ROUND, ALU.add, ALU.add)
                dve.drain()
                nc.vector.tensor_scalar(low[:, :, :], low[:, :, :], ROUND, None, ALU.subtract)
                dve.drain()
                nc.vector.scalar_tensor_tensor(rows_all[:, bass.ds(i, 1), :].rearrange("p b (t k) -> p (b t) k", k=TAPS),
                                               low[:, :, 0:TAPS], float(CELLS), low[:, :, TAPS:YX],
                                               ALU.mult, ALU.add).then_inc(rows_ready, 1)
                nc.vector.scalar_tensor_tensor(frac[:, :, :], yx[:, :, :], 1.0, low[:, :, :], ALU.add, ALU.subtract)
                dve.drain()
                nc.vector.tensor_scalar(rest[:, :, :], frac[:, :, :], -1.0, 1.0, ALU.mult, ALU.add)
                dve.wait_ge(mask_exp, i + 1)
                nc.vector.tensor_scalar(mask[:, :, :], mexp[:, :, :], 1.0, None, ALU.add)
                dve.drain()
                nc.vector.reciprocal(mask[:, :, :], mask[:, :, :])
                dve.drain()
                for dy, part in enumerate((rest, frac)):
                    nc.vector.tensor_tensor(wy[:, dy, :, :], part[:, :, 0:TAPS], mask[:, :, :], ALU.mult)
                dve.drain()
                for c in range(CORNERS):
                    part = (rest, frac)[c % 2]
                    to = corner_w[:, bass.ds(i, 1), :, :].rearrange("p b t (k c) -> p (b t k) c", c=CORNERS)[:, :, c]
                    last = nc.vector.tensor_tensor(to.rearrange("p (t k) -> p t k", k=TAPS), wy[:, c // 2, :, :],
                                                   part[:, :, TAPS:YX], ALU.mult)
                last.then_inc(corner_ready, 1)

            def l1_weigh(i, t):
                dve.wait_ge(got_sem[t], 16 * TAPS * (i + 1))
                w = corner_w[:, bass.ds(i, 1), t, :].rearrange("p b k -> p (b k)")
                nc.vector.tensor_tensor(weighed[:, :, :].rearrange("p k (c r) -> p (k c) r", r=R),
                                        got[:, t, :, :].rearrange("p k (c r) -> p (k c) r", r=R),
                                        w.rearrange("p (k a) -> p k a", a=1).to_broadcast([P, TAPS * CORNERS, R]),
                                        ALU.mult).then_inc(slot_free, 1)
                dve.drain()
                if t == TILES - 1:
                    dve.sem_inc(table_free, 1)

            def l1_add(i, t, early=False):
                if t >= 2 or early:
                    dve.wait_ge(st_mm, TILES * i + t - 1)
                nc.vector.tensor_reduce(samples[:, t % 2, :].rearrange("p (k r) -> p k r", r=R),
                                        weighed[:, :, :].rearrange("p k (c r) -> p k r c", r=R),
                                        axis=X, op=ALU.add).then_inc(sample_ready, 1)
                dve.drain()

            def l1_samples(i, t, early=False):
                l1_weigh(i, t)
                l1_add(i, t, early)

            def l1_conv2(i):
                dve.wait_ge(h2_high, 2 * i + 2)
                nc.vector.tensor_tensor(h2_stack[quarter(2, 2), :], h2_full[quarter(2, 2), :],
                                        h2_stack[quarter(2, 2), :].bitcast(fp32), ALU.subtract).then_inc(h2_split, 1)

            def l1_end(i):
                dve.wait_ge(w3_mm, i + 1)
                nc.vector.scalar_tensor_tensor(x2_sum[:, :], ys[:, :], bn_s[:, 2:3],
                                               xall[:, bass.ds(i, 1), :].rearrange("p b n -> p (b n)"),
                                               ALU.mult, ALU.add).then_inc(x2_added, 1)

            def l2_v(i):
                dve.wait_ge(v_mm[2], i + 1)
                nc.vector.tensor_tensor(vT[:, :, 0:C], xs[:, :].rearrange("p (j c) -> p j c", c=C),
                                        wt("bv2").rearrange("p (a c) -> p a c", a=1).to_broadcast([P, TILES, C]),
                                        ALU.add).then_inc(v_ready[2], 1)

            def l2_values(i, t):
                dve.wait_ge(o_mm[2], TILES * i + t + 1)
                bank = (xo, xp)[t % 2]
                nc.vector.reciprocal(inv[:, t:t + 1], bank[:, C:C + 1]).then_inc(inv2_done, 1)
                if t == TILES - 1:
                    dve.drain()
                    nc.vector.tensor_scalar(oT[:, t, :], bank[:, 0:C], inv[:, t:t + 1], None, ALU.mult)\
                        .then_inc(o_last, 1)

            def l2_end(i, h):
                dve.wait_ge(ot_mm, 2 * i + h + 1)
                if h == 0:
                    dve.wait_ge(x2_copied, i + 1)
                at = slice(h * HALF, (h + 1) * HALF)
                nc.vector.scalar_tensor_tensor(x3[:, at], xs[:, at], wt("gamma"),
                                               xall[:, bass.ds(i, 1), at].rearrange("p b n -> p (b n)"), ALU.mult,
                                               ALU.add)

            def l2_statistics(h):
                dve.drain()
                nc.vector.bn_stats(stats[:, h, :], x3[:, h * HALF:(h + 1) * HALF])

            def l3_moments(i):
                dve.drain()
                nc.vector.bn_aggr(mom[:, :], stats[:, :, :].rearrange("p h s -> p (h s)"))
                dve.drain()
                nc.vector.scalar_tensor_tensor(mom[:, 1:2], mom[:, 0:1], mom[:, 0:1], mom[:, 1:2], ALU.mult,
                                               ALU.add).then_inc(mom_ready, 1)

            def l3_norm(i):
                dve.wait_ge(g_mm, i + 1)
                nc.vector.tensor_copy(gmom[:, :], yo[:, 0:2])
                dve.drain()
                nc.vector.tensor_scalar(gsq[:, :], gmom[:, 0:1], gmom[:, 0:1], EPS, ALU.mult, ALU.subtract)
                dve.drain()
                nc.vector.tensor_tensor(gvar[:, :], gmom[:, 1:2], gsq[:, :], ALU.subtract).then_inc(gvar_ready, 1)
                dve.wait_ge(gstd_ready, i + 1)
                nc.vector.reciprocal(gscale[:, :], gstd[:, :])
                dve.drain()
                nc.vector.tensor_tensor(gscale[:, :], gscale[:, :], wt("gn_w"), ALU.mult)
                dve.drain()
                nc.vector.tensor_tensor(gbias[:, :], gmom[:, 0:1], gscale[:, :], ALU.mult)
                dve.drain()
                nc.vector.tensor_tensor(gbias[:, :], wt("gn_b"), gbias[:, :], ALU.subtract).then_inc(gaff_ready, 1)

            def l3_values_in(i):
                dve.wait_ge(v3_mm, i + 1)
                nc.vector.tensor_tensor(v3T[:, :, :], yy[:, :].rearrange("p (j c) -> p j c", c=C),
                                        bvp3[:, :].rearrange("p (a c) -> p a c", a=1).to_broadcast([P, TILES, C]),
                                        ALU.add).then_inc(v3_ready, 1)

            def l3_max(i, t, pair):
                dve.wait_ge(s3_mm, TILES * i + t + 1)
                nc.vector.tensor_reduce(neg_max3[:, t:t + 1], pair[:, :], axis=X, op=ALU.max,
                                        negate=True).then_inc(max3_done, 1)

            def l3_turn(i, t):
                dve.wait_ge(pt_mm, 2 * TILES * i + 2 * t + 1)
                nc.vector.tensor_copy(probsT[:, 0:HALF], yt[:, :]).then_inc(pt_dve, 1)

            def l3_inverse(i, t):
                dve.wait_ge(exp3_done, TILES * i + t + 1)
                nc.vector.reciprocal(inv3[:, t:t + 1], denom3[:, t:t + 1]).then_inc(inv3_done, 1)

            def l3_end(i, h=None):
                dve.wait_ge(ot3_mm, i + 1 + (h or 0))
                dve.wait_ge(h3_ready, 2 * i + 2)
                at = slice(0, N) if h is None else slice(h * HALF, (h + 1) * HALF)
                nc.vector.scalar_tensor_tensor(y[:, at], ys[:, at], 2.0 ** -0.5, x3s[:, at], ALU.mult,
                                               ALU.add).then_inc(y_ready, 1)

            def first_loop_step(a, b, following, samples_too=False):
                for t in range(TILES):
                    maximum(0, a, t, (xs, ys)[t % 2])
                shift_parts(0, a)
                if b is not None:
                    l1_coordinates(b, xp)
                l0_denominators(a, samples_too)
                l0_end(a)
                if following is not None:
                    l0_project(following)

            def second_loop_step(a, b, c):
                L3, L2, SAMPLES = a is not None, b is not None, c is not None
                if L3:
                    l3_moments(a)
                    l3_norm(a)
                if L2:
                    low_part(q_stack, 2, ys, b + 1, wt("bq2")[quarter(2), :], q_high[2], q_ready[2])
                    low_part(k_stack, 1, xq, b + 1, wt("bk2")[quarter(1), :], k_high[2], k_ready[2])
                    l2_v(b)
                if L3:
                    l3_max(a, 0, ys)
                    l3_values_in(a)
                if L2:
                    maximum(2, b, 0, xq)
                start = 3 if L3 else 1
                for t in range(TILES):
                    if L3:
                        l3_turn(a, t)
                    if L2 and t == 0:
                        maximum(2, b, 1, xs)
                    if SAMPLES and t >= 3:
                        l1_weigh(c, t - start)
                    if L3:
                        if t + 1 < TILES:
                            l3_max(a, t + 1, (ys if L2 else (ys, xs)[(t + 1) % 2]))
                        l3_inverse(a, t)
                    if L2 and t < 3:
                        maximum(2, b, 2 * t + 2, xq)
                        maximum(2, b, 2 * t + 3, xs)
                    if SAMPLES and t >= 3:
                        l1_add(c, t - start)
                    if L2 and t == 2:
                        shift_parts(2, b)
                    if L2 and t == 7:
                        l2_values(b, 0)
                        l2_values(b, 1)
                if SAMPLES:
                    l1_samples(c, TILES - start)
                if L3 and L2:
                    l3_end(a)
                elif L3:
                    for h in range(2):
                        l3_end(a, h)
                if L2:
                    for n in range(2, TILES):
                        l2_values(b, n)
                        if SAMPLES and L3:
                            if n == 2:
                                l1_samples(c, 6)
                            if n == 3:
                                l1_weigh(c, 7)
                            if n == 4:
                                l1_add(c, 7)
                            if n == 5:
                                l1_conv2(c)
                            if n == 6:
                                l1_end(c)
                        if SAMPLES and not L3 and n == 5:
                            l1_conv2(c)
                        if SAMPLES and not L3 and n == 6:
                            l1_end(c)
                        if n == 6:
                            l2_end(b, 0)
                    l2_statistics(0)
                    l2_end(b, 1)
                    l2_statistics(1)

            nc.vector.memset(cells[:, :, :], 0.0)
            nc.vector.memset(shift[:, :, :], 0.0)
            nc.vector.memset(vT[:, :, C:C + 1], 1.0)
            dve.sem_inc(slot_free, TILES)
            dve.sem_inc(table_free, 2)
            dve.sem_inc(y_ready, 1)
            dve.sem_inc(y_out, 16)
            dve.wait_ge(weights0_in, 16)
            nc.vector.tensor_copy(ident16[:, :], ident)
            nc.vector.tensor_copy(k_stack[quarter(3), :], wt("ones")[quarter(3), :].to_broadcast([R, N]))
            dve.wait_ge(x_in[0], 16)
            nc.vector.tensor_copy(xcur[:, :], xall[:, 0, :]).then_inc(x_ready[0], 1)
            l0_project(0)
            first_loop_step(0, None, 1)
            dve.wait_ge(weights_in, 16)
            nc.vector.tensor_scalar(bn_std[:, :], wt("bn_v"), EPS, None, ALU.add).then_inc(setup_dve, 1)
            nc.vector.tensor_copy(w3_stack[:, :], wt("w3"))
            nc.vector.tensor_scalar(bq3s[:, :], wt("bq3"), float(C) ** -0.5, None, ALU.mult)
            nc.vector.tensor_scalar(bp3s[:, :], wt("bp3"), 2.0 ** -0.5, None, ALU.mult)
            dve.drain()
            for c in (1, 3):
                nc.vector.tensor_tensor(w3_stack[quarter(c), :], wt("w3")[quarter(c), :],
                                        w3_stack[quarter(c), :].bitcast(fp32), ALU.subtract)
            dve.wait_ge(setup_sqrt, 1)
            nc.vector.reciprocal(bn_s[:, :], bn_std[:, :])
            dve.drain()
            nc.vector.tensor_tensor(bn_s[:, :], bn_s[:, :], wt("bn_g"), ALU.mult)
            dve.drain()
            nc.vector.tensor_tensor(bn_t[:, :], wt("bn_m"), bn_s[:, :], ALU.mult)
            dve.drain()
            nc.vector.tensor_tensor(bn_t[:, :], wt("bn_b"), bn_t[:, :], ALU.subtract)
            dve.drain()
            nc.vector.scalar_tensor_tensor(bn_t[:, 1:2], bn_s[:, 1:2], wt("dcn_b"), bn_t[:, 1:2], ALU.mult,
                                           ALU.add).then_inc(setup_dve, 1)
            for b in range(1, BATCH):
                dve.wait_ge(x_in[b], 16)
            with dve.Fori(0, BATCH - 2) as i:
                first_loop_step(i + 1, i, i + 2)
            dve.wait_ge(corner_ready, 1)
            first_loop_step(BATCH - 1, BATCH - 2, None, samples_too=True)
            for t in range(4, TILES):
                l1_samples(0, t)
            for t in range(2):
                l1_samples(1, t, early=True)
            l1_conv2(0)
            l1_end(0)
            l1_coordinates(BATCH - 1, xp)
            second_loop_step(None, 0, 1)
            with dve.Fori(0, BATCH - 2) as i:
                second_loop_step(i, i + 1, i + 2)
            second_loop_step(BATCH - 2, BATCH - 1, None)
            second_loop_step(BATCH - 1, None, None)


def pack(a):
    w = np.zeros((P, WIDTH), np.float32)

    def put(name, value):
        value = np.asarray(value, np.float32)
        value = value.reshape(value.shape[0], -1)
        w[:value.shape[0], AT[name][0]:AT[name][1]] = value

    def column(v):
        return np.asarray(v).reshape(-1, 1)

    four = lambda v: np.concatenate([v] * 4, axis=0)
    put("ident", np.eye(P))
    put("wq0", four(a["L0_conv_Wq"]).T)
    put("wk0", four(a["L0_conv_Wk"]).T)
    put("wv0", a["L0_conv_Wv"].T)
    put("wp0", four(a["L0_conv_Wp"].T))
    put("ones", (np.arange(P) // 2 == 3 * R // 2)[:, None])
    put("ones0", np.ones((P, R)))
    put("dsum", (np.arange(P) % R == 0)[:, None])
    put("w1", four(a["L1_conv_w1"]).T)
    for n, (name, k) in enumerate((("bn_g", "g"), ("bn_b", "b"), ("bn_m", "m"), ("bn_v", "v"))):
        put(name, np.concatenate([column(four(a[f"L1_conv_bn1_{k}"])), column(four(a[f"L1_conv_bn2_{k}"])),
                                  column(a[f"L1_conv_bn3_{k}"])], axis=1))
    put("dcn_b", column(four(a["L1_conv_dcn_b"])))
    order = [2 * k for k in range(TAPS)] + [2 * k + 1 for k in range(TAPS)] + list(range(YX, OFFS))
    woff = a["L1_conv_woff"][order]
    to = np.zeros((CORNERS, R, 4, R), np.float32)
    for n, (oy, ox) in enumerate(PLACES):
        for c in range(CORNERS):
            ky, kx = oy + c // 2, ox + c % 2
            if (oy == 0 or ky == 2) and (ox == 0 or kx == 2):
                to[c, :, n, :OFFS] = woff[:, :, ky, kx].T
    put("woff", to.reshape(P, -1))
    put("boff", column(a["L1_conv_boff"][order]))
    put("osum", np.concatenate([np.eye(R, OFFS)] * 4, axis=0))
    p, t, k = np.arange(P)[:, None, None], np.arange(TILES)[None, :, None], np.arange(TAPS)[None, None, :]
    by, bx = t * ROWS + p // W - 1 + k // 3, p % W - 1 + k % 3 + 0 * t
    put("base", np.concatenate([by, bx], axis=2))
    w2 = a["L1_conv_w2"].reshape(R, R, TURNS, TAPS_A_TURN).transpose(3, 1, 2, 0)
    put("w2", np.concatenate([w2] * 4, axis=3).reshape(TR, TURNS * P))
    put("w3", four(a["L1_conv_w3"].T))
    pad = lambda v: four(np.concatenate([v, np.zeros((R - QK2,) + v.shape[1:], np.float32)], axis=0))
    put("wq2", pad(a["L2_conv_wq"]).T)
    put("wk2", pad(a["L2_conv_wk"]).T)
    put("wv2", a["L2_conv_wv"].T)
    put("bq2", column(pad(a["L2_conv_bq"])))
    put("bk2", column(pad(a["L2_conv_bk"])))
    put("bv2", np.broadcast_to(a["L2_conv_bv"], (P, C)))
    put("gamma", column(a["L2_conv_gamma"]))
    put("wq3", a["L3_conv_Wq"])
    put("wk3", a["L3_conv_Wk"])
    put("wvT3", a["L3_conv_Wv"].T)
    put("wp3", a["L3_conv_Wp"])
    for k in ("bq", "bk", "bp"):
        put(k + "3", column(a["L3_conv_" + k]))
    put("bv3", np.broadcast_to(column(a["L3_conv_bv"]), (C, P)))
    put("gn_w", column(a["L3_conv_gn_w"]))
    put("gn_b", column(a["L3_conv_gn_b"]))
    put("gavg", np.kron(np.eye(C // GROUP), np.full((GROUP, GROUP), 1.0 / GROUP)))
    return w


def kernel(**inputs):
    import concourse.bacc as bacc
    from concourse.bass_utils import run_bass_kernel_spmd

    a = {k: np.asarray(v) for k, v in inputs.items()}
    x, w = np.ascontiguousarray(a["x"]), pack(a)
    nc = bacc.Bacc("TRN2", target_bir_lowering=False, num_devices=1)
    fp32 = mybir.dt.float32
    x_ap = nc.dram_tensor("x_dram", x.shape, fp32, kind="ExternalInput").ap()
    w_ap = nc.dram_tensor("weights_dram", w.shape, fp32, kind="ExternalInput").ap()
    o_ap = nc.dram_tensor("out_dram", x.shape, fp32, kind="ExternalOutput").ap()
    build(nc, x_ap, w_ap, o_ap)
    result = run_bass_kernel_spmd(nc, [{"x_dram": x, "weights_dram": w}], core_ids=[0])
    return result.results[0]["out_dram"]
```
